# Optimizing a Trainium2 kernel written in Bass

```python
import numpy as np
import jax
import jax.numpy as jnp

def _softmax(x, axis=-1):
    return jax.nn.softmax(x, axis=axis)

def _gelu(x):
    return jax.nn.gelu(x, approximate=True)

def _silu(x):
    return jax.nn.silu(x)

def _sigmoid(x):
    return jax.nn.sigmoid(x)

def _layernorm(x, axis=-1, eps=1e-05):
    m = jnp.mean(x, axis=axis, keepdims=True)
    v = jnp.var(x, axis=axis, keepdims=True)
    return (x - m) / jnp.sqrt(v + eps)

def _scatter_add(tgt, idx, src, axis=0):
    return tgt.at[idx].add(src)

def _segment_sum(src, seg, n):
    return jax.ops.segment_sum(src, seg, n)
kernel_name = 'mk_adj_ffn_d2_adj_r2_2003b8'

def setup_inputs(seed: int=0):
    np.random.seed(seed)
    _w = jnp.asarray

    def _rec_inputs():
        import jax
        import jax.numpy as jnp
        _gk = jax.random.key(seed)
        x = -0.000929 + 1 * jax.random.normal(jax.random.fold_in(_gk, 1), (4096, 128), jnp.float32)
        _a = jax.random.bernoulli(jax.random.fold_in(_gk, 2), 0.00390625, (4096, 4096))
        _a = jnp.logical_or(_a, jnp.swapaxes(_a, -1, -2))
        _a = jnp.logical_or(_a, jnp.eye(4096, dtype=bool))
        _af = _a.astype(jnp.float32)
        _af = _af * jax.random.uniform(jax.random.fold_in(_gk, 3), (4096, 4096), jnp.float32, 0.05, 1)
        adj = _af
        return (x, adj)
    x, adj = _rec_inputs()

    def _L0_gnn_setup():
        import jax, jax.numpy as jnp
        import numpy as np
        N, H, HEADS = (2048, 128, 3)
        ALPHA = 0.2
        NEG_INF = -9000000000000000.0

        def _sign_adj(key, n, density):
            k1, k2 = jax.random.split(key)
            mask = jax.random.uniform(k1, (n, n)) < density
            sign = jnp.where(jax.random.uniform(k2, (n, n)) < 0.5, -1.0, 1.0)
            adj = jnp.where(mask, sign, 0.0).astype(jnp.float32)
            idx = jnp.arange(n)
            return adj.at[idx, idx].set(1.0)

        def _gru_cell(x, hstate, Wih, Whh, bih, bhh):
            gi = x @ Wih.T + bih
            gh = hstate @ Whh.T + bhh
            ir, iz, inn = jnp.split(gi, 3, axis=1)
            hr, hz, hn = jnp.split(gh, 3, axis=1)
            r = jax.nn.sigmoid(ir + hr)
            z = jax.nn.sigmoid(iz + hz)
            n = jnp.tanh(inn + r * hn)
            return (1.0 - z) * n + z * hstate

        def _gat_head(h, node_adj, edge_adj, W, a):
            hW = h @ W
            hp = (node_adj > 0).astype(hW.dtype) @ hW
            hm = (node_adj < 0).astype(hW.dtype) @ hW
            e_plus = jax.nn.leaky_relu(jnp.concatenate([hp, hm], axis=1) @ a, ALPHA)[:, 0]
            e_minus = jax.nn.leaky_relu(jnp.concatenate([hm, hp], axis=1) @ a, ALPHA)[:, 0]
            att = jnp.where(edge_adj > 0, e_plus[None, :], NEG_INF)
            att = jnp.where(edge_adj < 0, e_minus[None, :], att)
            att = jax.nn.softmax(att, axis=1)
            return att * edge_adj @ hW
        key = jax.random.key(seed)
        ks = jax.random.split(key, 16)
        std = 0.01
        gain = 1.414
        return {'h': jax.random.normal(ks[0], (N, H), jnp.float32), 'node_adj': _sign_adj(ks[1], N, 0.005), 'edge_adj': _sign_adj(ks[2], N, 0.005), 'gat_W': jax.random.normal(ks[3], (HEADS, H, H), jnp.float32) * (gain / np.sqrt(H, dtype=np.float32)), 'gat_a': jax.random.normal(ks[4], (HEADS, 2 * H, 1), jnp.float32) * 0.1, 'edge_Wih': jax.random.normal(ks[5], (3 * H, H), jnp.float32) * std, 'edge_Whh': jax.random.normal(ks[6], (3 * H, H), jnp.float32) * std, 'edge_bih': jnp.zeros((3 * H,), jnp.float32), 'edge_bhh': jnp.zeros((3 * H,), jnp.float32), 'node_Wih': jax.random.normal(ks[7], (3 * H, H), jnp.float32) * std, 'node_Whh': jax.random.normal(ks[8], (3 * H, H), jnp.float32) * std, 'node_bih': jnp.zeros((3 * H,), jnp.float32), 'node_bhh': jnp.zeros((3 * H,), jnp.float32)}
    _L0_gnn_all = _L0_gnn_setup()
    _L0_gnn_in = {k: v for k, v in _L0_gnn_all.items() if k in ('gat_W', 'gat_a', 'edge_Wih', 'edge_Whh', 'edge_bih', 'edge_bhh', 'node_Wih', 'node_Whh', 'node_bih', 'node_bhh')}
    del _L0_gnn_all

    def _L0_ffn_setup():
        import jax, jax.numpy as jnp
        import numpy as np
        B, S, D, F, E, K = (8, 1024, 128, 512, 8, 2)
        key = jax.random.key(seed)
        ks = jax.random.split(key, 10)
        s = 0.02
        return {'x': jax.random.normal(ks[0], (B, S, D), dtype=jnp.float32), 'Wr': jax.random.normal(ks[1], (D, E), dtype=jnp.float32) * s, 'W1s': jax.random.normal(ks[2], (D, F), dtype=jnp.float32) * s, 'b1s': jnp.zeros((F,), dtype=jnp.float32), 'W2s': jax.random.normal(ks[3], (F, D), dtype=jnp.float32) * s, 'b2s': jnp.zeros((D,), dtype=jnp.float32), 'W1p': jax.random.normal(ks[4], (E, D, F), dtype=jnp.float32) * s, 'b1p': jnp.zeros((E, F), dtype=jnp.float32), 'W2p': jax.random.normal(ks[5], (E, F, D), dtype=jnp.float32) * s, 'b2p': jnp.zeros((E, D), dtype=jnp.float32)}
    _L0_ffn_all = _L0_ffn_setup()
    _L0_ffn_in = {k: v for k, v in _L0_ffn_all.items() if k in ('Wr', 'W1s', 'b1s', 'W2s', 'b2s', 'W1p', 'b1p', 'W2p', 'b2p')}
    del _L0_ffn_all

    def _L1_gnn_setup():
        import jax, jax.numpy as jnp
        import numpy as np
        N = 10000
        D = 128
        F = 128
        K = F // 8
        key = jax.random.key(seed)
        k1, k2, k3, k4, k5 = jax.random.split(key, 5)
        h = jax.random.normal(k1, (N, D), dtype=jnp.float32)
        adj = jax.random.uniform(k2, (N, N), dtype=jnp.float32)
        W1 = jax.random.normal(k3, (D, K), dtype=jnp.float32) * 0.05
        W2 = jax.random.normal(k4, (K, D, F), dtype=jnp.float32) * 0.05
        b = jax.random.normal(k5, (K, F), dtype=jnp.float32) * 0.05
        return {'h': h, 'adj': adj, 'W1': W1, 'W2': W2, 'b': b}
    _L1_gnn_all = _L1_gnn_setup()
    _L1_gnn_in = {k: v for k, v in _L1_gnn_all.items() if k in ('W1', 'W2', 'b')}
    del _L1_gnn_all

    def _L1_ffn_setup():
        import jax, jax.numpy as jnp
        import numpy as np
        D_MODEL = 128
        EXPERT_DIM = 256
        NUM_EXPERTS = 8
        TOP_K = 2
        SEQ_LEN = 1024
        BATCH = 2
        key = jax.random.key(seed)
        ks = jax.random.split(key, 8)
        s = 0.02
        x = jax.random.normal(ks[0], (SEQ_LEN, BATCH, D_MODEL), dtype=jnp.float32)
        Wg = jax.random.normal(ks[1], (D_MODEL, NUM_EXPERTS), dtype=jnp.float32) * s
        bg = jax.random.normal(ks[2], (NUM_EXPERTS,), dtype=jnp.float32) * s
        bias = jnp.zeros((NUM_EXPERTS,), dtype=jnp.float32)
        W1 = jax.random.normal(ks[3], (NUM_EXPERTS, D_MODEL, EXPERT_DIM), dtype=jnp.float32) * s
        b1 = jax.random.normal(ks[4], (NUM_EXPERTS, EXPERT_DIM), dtype=jnp.float32) * s
        W2 = jax.random.normal(ks[5], (NUM_EXPERTS, EXPERT_DIM, D_MODEL), dtype=jnp.float32) * s
        b2 = jax.random.normal(ks[6], (NUM_EXPERTS, D_MODEL), dtype=jnp.float32) * s
        return {'x': x, 'Wg': Wg, 'bg': bg, 'bias': bias, 'W1': W1, 'b1': b1, 'W2': W2, 'b2': b2}
    _L1_ffn_all = _L1_ffn_setup()
    _L1_ffn_in = {k: v for k, v in _L1_ffn_all.items() if k in ('Wg', 'bg', 'bias', 'W1', 'b1', 'W2', 'b2')}
    del _L1_ffn_all
    return {'x': x, 'adj': adj, 'L0_gnn_gat_W': _L0_gnn_in['gat_W'], 'L0_gnn_gat_a': _L0_gnn_in['gat_a'], 'L0_gnn_edge_Wih': _L0_gnn_in['edge_Wih'], 'L0_gnn_edge_Whh': _L0_gnn_in['edge_Whh'], 'L0_gnn_edge_bih': _L0_gnn_in['edge_bih'], 'L0_gnn_edge_bhh': _L0_gnn_in['edge_bhh'], 'L0_gnn_node_Wih': _L0_gnn_in['node_Wih'], 'L0_gnn_node_Whh': _L0_gnn_in['node_Whh'], 'L0_gnn_node_bih': _L0_gnn_in['node_bih'], 'L0_gnn_node_bhh': _L0_gnn_in['node_bhh'], 'L0_ffn_Wr': _L0_ffn_in['Wr'], 'L0_ffn_W1s': _L0_ffn_in['W1s'], 'L0_ffn_b1s': _L0_ffn_in['b1s'], 'L0_ffn_W2s': _L0_ffn_in['W2s'], 'L0_ffn_b2s': _L0_ffn_in['b2s'], 'L0_ffn_W1p': _L0_ffn_in['W1p'], 'L0_ffn_b1p': _L0_ffn_in['b1p'], 'L0_ffn_W2p': _L0_ffn_in['W2p'], 'L0_ffn_b2p': _L0_ffn_in['b2p'], 'L1_gnn_W1': _L1_gnn_in['W1'], 'L1_gnn_W2': _L1_gnn_in['W2'], 'L1_gnn_b': _L1_gnn_in['b'], 'L1_ffn_Wg': _L1_ffn_in['Wg'], 'L1_ffn_bg': _L1_ffn_in['bg'], 'L1_ffn_bias': _L1_ffn_in['bias'], 'L1_ffn_W1': _L1_ffn_in['W1'], 'L1_ffn_b1': _L1_ffn_in['b1'], 'L1_ffn_W2': _L1_ffn_in['W2'], 'L1_ffn_b2': _L1_ffn_in['b2']}

def reference(x, adj, L0_gnn_gat_W, L0_gnn_gat_a, L0_gnn_edge_Wih, L0_gnn_edge_Whh, L0_gnn_edge_bih, L0_gnn_edge_bhh, L0_gnn_node_Wih, L0_gnn_node_Whh, L0_gnn_node_bih, L0_gnn_node_bhh, L0_ffn_Wr, L0_ffn_W1s, L0_ffn_b1s, L0_ffn_W2s, L0_ffn_b2s, L0_ffn_W1p, L0_ffn_b1p, L0_ffn_W2p, L0_ffn_b2p, L1_gnn_W1, L1_gnn_W2, L1_gnn_b, L1_ffn_Wg, L1_ffn_bg, L1_ffn_bias, L1_ffn_W1, L1_ffn_b1, L1_ffn_W2, L1_ffn_b2):
    import jax
    import jax.numpy as jnp

    def _L0_gnn_ref(h, node_adj, edge_adj, gat_W, gat_a, edge_Wih, edge_Whh, edge_bih, edge_bhh, node_Wih, node_Whh, node_bih, node_bhh):
        import jax, jax.numpy as jnp
        import numpy as np
        N, H, HEADS = (2048, 128, 3)
        ALPHA = 0.2
        NEG_INF = -9000000000000000.0

        def _sign_adj(key, n, density):
            k1, k2 = jax.random.split(key)
            mask = jax.random.uniform(k1, (n, n)) < density
            sign = jnp.where(jax.random.uniform(k2, (n, n)) < 0.5, -1.0, 1.0)
            adj = jnp.where(mask, sign, 0.0).astype(jnp.float32)
            idx = jnp.arange(n)
            return adj.at[idx, idx].set(1.0)

        def _gru_cell(x, hstate, Wih, Whh, bih, bhh):
            gi = x @ Wih.T + bih
            gh = hstate @ Whh.T + bhh
            ir, iz, inn = jnp.split(gi, 3, axis=1)
            hr, hz, hn = jnp.split(gh, 3, axis=1)
            r = jax.nn.sigmoid(ir + hr)
            z = jax.nn.sigmoid(iz + hz)
            n = jnp.tanh(inn + r * hn)
            return (1.0 - z) * n + z * hstate

        def _gat_head(h, node_adj, edge_adj, W, a):
            hW = h @ W
            hp = (node_adj > 0).astype(hW.dtype) @ hW
            hm = (node_adj < 0).astype(hW.dtype) @ hW
            e_plus = jax.nn.leaky_relu(jnp.concatenate([hp, hm], axis=1) @ a, ALPHA)[:, 0]
            e_minus = jax.nn.leaky_relu(jnp.concatenate([hm, hp], axis=1) @ a, ALPHA)[:, 0]
            att = jnp.where(edge_adj > 0, e_plus[None, :], NEG_INF)
            att = jnp.where(edge_adj < 0, e_minus[None, :], att)
            att = jax.nn.softmax(att, axis=1)
            return att * edge_adj @ hW
        dn = jnp.diag(node_adj)
        de = jnp.diag(edge_adj)
        idx = jnp.arange(node_adj.shape[0])
        node_adj_norm = node_adj.at[idx, idx].add(-dn)
        edge_adj_norm = edge_adj.at[idx, idx].add(-de)
        node_support = node_adj_norm @ h
        edge_output = _gru_cell(node_support, h, edge_Wih, edge_Whh, edge_bih, edge_bhh)
        edge_support = _gat_head(h, node_adj_norm, edge_adj_norm, gat_W[0], gat_a[0])
        for i in range(1, HEADS):
            edge_support = edge_support + _gat_head(h, node_adj_norm, edge_adj_norm, gat_W[i], gat_a[i])
        edge_support = edge_support / HEADS
        node_output = _gru_cell(edge_support, h, node_Wih, node_Whh, node_bih, node_bhh)
        return de[:, None] * edge_output + dn[:, None] * node_output

    def _L0_ffn_ref(x, Wr, W1s, b1s, W2s, b2s, W1p, b1p, W2p, b2p):
        import jax, jax.numpy as jnp
        import numpy as np
        B, S, D, F, E, K = (8, 1024, 128, 512, 8, 2)
        gelu = lambda t: jax.nn.gelu(t, approximate=False)
        shared = gelu(x @ W1s + b1s) @ W2s + b2s
        rw = jax.nn.softmax(x @ Wr, axis=-1)
        topw, topi = jax.lax.top_k(rw, K)
        topw = topw / jnp.sum(topw, axis=-1, keepdims=True)
        mask = jnp.sum(jax.nn.one_hot(topi, E, dtype=topw.dtype) * topw[..., None], axis=-2)
        h = gelu(jnp.einsum('bsd,edf->bsef', x, W1p) + b1p)
        priv = jnp.einsum('bsef,efd->bsed', h, W2p) + b2p
        routed = jnp.einsum('bsed,bse->bsd', priv, mask)
        return shared + routed

    def _L1_gnn_ref(h, adj, W1, W2, b):
        import jax, jax.numpy as jnp
        import numpy as np
        N = 10000
        D = 128
        F = 128
        K = F // 8
        node = h @ W1
        hw = jnp.einsum('nc,kcf->nkf', h, W2)
        x = jnp.einsum('nk,nkf->nf', node, hw)
        x = adj @ x
        x = x + node @ b
        return jax.nn.relu(x)

    def _L1_ffn_ref(x, Wg, bg, bias, W1, b1, W2, b2):
        import jax, jax.numpy as jnp
        import numpy as np
        D_MODEL = 128
        EXPERT_DIM = 256
        NUM_EXPERTS = 8
        TOP_K = 2
        SEQ_LEN = 1024
        BATCH = 2
        x_flat = x.reshape(-1, D_MODEL)
        gate_logits = x_flat @ Wg + bg + bias
        topk_vals, topk_idx = jax.lax.top_k(gate_logits, TOP_K)
        topk_w = jax.nn.softmax(topk_vals, axis=-1)
        combine = (jax.nn.one_hot(topk_idx, NUM_EXPERTS, dtype=x.dtype) * topk_w[..., None]).sum(axis=1)
        h = jax.nn.relu(jnp.einsum('td,edh->teh', x_flat, W1) + b1)
        y = jnp.einsum('teh,ehd->ted', h, W2) + b2
        out = jnp.einsum('ted,te->td', y, combine)
        return out.reshape(x.shape)
    x = x + _L0_gnn_ref(_layernorm(x, axis=-1), adj, adj, L0_gnn_gat_W, L0_gnn_gat_a, L0_gnn_edge_Wih, L0_gnn_edge_Whh, L0_gnn_edge_bih, L0_gnn_edge_bhh, L0_gnn_node_Wih, L0_gnn_node_Whh, L0_gnn_node_bih, L0_gnn_node_bhh)
    x = x + _L0_ffn_ref(_layernorm(x, axis=-1)[None], L0_ffn_Wr, L0_ffn_W1s, L0_ffn_b1s, L0_ffn_W2s, L0_ffn_b2s, L0_ffn_W1p, L0_ffn_b1p, L0_ffn_W2p, L0_ffn_b2p)[0]
    x = x + _L1_gnn_ref(_layernorm(x, axis=-1), adj, L1_gnn_W1, L1_gnn_W2, L1_gnn_b)
    x = x + _L1_ffn_ref(_layernorm(x, axis=-1)[None], L1_ffn_Wg, L1_ffn_bg, L1_ffn_bias, L1_ffn_W1, L1_ffn_b1, L1_ffn_W2, L1_ffn_b2)[0]
    return x

_drawn_inputs = setup_inputs


def setup_inputs(seed=0):
    import zlib

    import numpy as np

    out = dict(_drawn_inputs(seed))
    spreads = {'L0_gnn_edge_bih': (0.0, 0.313),
     'L0_gnn_edge_bhh': (0.0, 0.447),
     'L0_gnn_node_bih': (0.0, 0.292),
     'L0_gnn_node_bhh': (0.0, 0.439),
     'L0_ffn_b1s': (0.0, 0.385),
     'L0_ffn_b2s': (0.0, 0.1),
     'L0_ffn_b1p': (0.0, 0.507),
     'L0_ffn_b2p': (0.0, 0.1),
     'L1_ffn_bias': (0.0, 0.8)}
    factors = {'L0_gnn_gat_W': 4.385,
     'L0_gnn_gat_a': 4.601,
     'L0_gnn_edge_Whh': 3.099,
     'L0_gnn_node_Wih': 4.403,
     'L0_gnn_node_Whh': 2.936,
     'L1_ffn_Wg': 6.239,
     'L1_ffn_bg': 8.0,
     'L1_ffn_W1': 7.142,
     'L1_ffn_b1': 8.0,
     'L1_ffn_W2': 5.987,
     'L1_ffn_b2': 8.0}
    for name, (base, spread) in spreads.items():
        noise = np.random.default_rng([zlib.crc32(name.encode()), seed]).standard_normal(out[name].shape)
        drawn = base * np.exp(spread * noise) if base else spread * noise
        out[name] = jnp.asarray(drawn.astype(out[name].dtype))
    for name, factor in factors.items():
        out[name] = (out[name] * factor).astype(out[name].dtype)
    return out
```

```python
import math
from contextlib import ExitStack

import concourse.bass as bass
from concourse import mybir

F32, BF16, FP16 = mybir.dt.float32, mybir.dt.bfloat16, mybir.dt.float16
I32, I16, U8 = mybir.dt.int32, mybir.dt.int16, mybir.dt.uint8
BYTES = {F32: 4, BF16: 2, FP16: 2, I32: 4, I16: 2, U8: 1}
ALU = mybir.AluOpType
ACT = mybir.ActivationFunctionType
AX = mybir.AxisListType.X
ROP = bass.bass_isa.ReduceOp
ds = bass.ds

P = 128
N = 4096
NT = N // P
CH = 512
NC = N // CH
HEADS = 3
RB = 1024
NRB = N // RB
TPB = RB // P
LEVEL = 64
KL = 21
PART = KL * HEADS
POISON = float(2.0 ** 60)
CLEAN = float(2.0 ** 40)
LN2 = math.log(2.0)
LN2_HI = 355.0 / 512.0
LN2_LO = LN2 - LN2_HI
ROUND = float(1.5 * 2 ** 23)
TINY = 1e-30
EPS = 1e-5
SLOPE = 0.2
K1 = 16
NE = 8
FFN0 = (9, 4)
FFN1 = (8, 2)

C_ID, C_OFF, C_ONE, C_SD, C_SC, C_KK, C_PR, C_SG, C_END = 0, 128, 256, 384, 390, 396, 417, 425, 427

SCRATCH = "Internal"
STOP = 99


def build(nc, a, out):
    with ExitStack() as ctx:
        base = (nc.sbuf_base + 63) // 64 * 64
        KB = 1024
        small = [base]
        R = base + 6 * KB

        def sb(name, shape, dt, kb=None):
            size = BYTES[dt] * math.prod(shape[1:])
            if kb is None:
                off = small[0]
                small[0] = (off + size + 63) // 64 * 64
                assert small[0] <= R
            else:
                off = R + int(kb * KB)
            return nc.alloc_sbuf_tensor_at(name, shape, dt, offset=off)

        def sem(name):
            return ctx.enter_context(nc.semaphore(name))

        def dram(name, shape, dt):
            return nc.dram_tensor(name, shape, dt, kind=SCRATCH).ap()

        class Chain:

            def __init__(self, eng, s, start=0):
                self.eng, self.s, self.start, self.n = eng, s, start, 0

            def link(self, ins):
                ins.then_inc(self.s, 1)
                self.n += 1
                self.eng.wait_ge(self.s, self.start + self.n)

        cst = sb("cst", [P, C_END], F32)
        ident, offd = cst[:, C_ID:C_ID + P], cst[:, C_OFF:C_OFF + P]
        ones = cst[:, C_ONE:C_ONE + P]
        selD, selCf = cst[:, C_SD:C_SD + 6], cst[:, C_SC:C_SC + 6]
        kk, prio = cst[:, C_KK:C_KK + KL], cst[:, C_PR:C_PR + NE]
        sgn = cst[:, C_SG:C_SG + 2]
        selC = sb("selC", [P, 6], BF16)
        dpt = sb("dpt", [P, 2 * NT * HEADS], F32)
        wm = sb("wm", [P, 2 * NT * HEADS], F32)
        lev = sb("lev", [P, KL], F32)
        nsg = sb("nsg", [P, 3], I32)
        sm = sb("sm", [P, 16], F32)
        stat = sb("stat", [P, 6, NT], F32)
        zero = sb("zero", [P, CH], BF16)

        xT = sb("xT", [P, N], F32, 0)
        hT = sb("hT", [P, N], F32, 16)
        hn = sb("hn", [P, NT, P], F32, 32)
        sq = sb("sq", [P, NT // 2, P], F32, 48)
        gwTt = sb("gwTt", [P, HEADS * P], F32, 56)
        ga = sb("ga", [P, HEADS, 2], F32, 58)
        wa = sb("wa", [P, 2, HEADS], F32, 58.25)
        uvr = sb("uvr", [P, NT, 6], F32, 59)
        keep = sb("keep", [P, NT * N], U8, 0)
        Pb = [sb(f"Pb{i}", [P, N], BF16, 128 + 8 * i) for i in range(2)]
        Ar = [sb(f"Ar{i}", [P, N], F32, 144 + 16 * i) for i in range(2)]
        junk = sb("junk", [P, N], BF16, 176)
        uvs = sb("uvs", [P, NT, 3, 6], BF16, 184)
        uvx = sb("uvx", [P, NT, 3, 6], BF16, 186)
        negs = sb("negs", [P, NT], F32, 188)
        zs = sb("zs", [P, NT, 18], F32, 144)
        z6 = sb("z6", [P, NT, 6], F32, 147)
        e6 = sb("e6", [P, 2, NT * HEADS], F32, 148)
        q6 = sb("q6", [P, 2, NT * HEADS], F32, 149)
        f6 = sb("f6", [P, 2, NT * HEADS], F32, 150)
        lvU = sb("lvU", [P, NT * HEADS, KL], F32, 144)
        lvE = sb("lvE", [P, NT * HEADS, KL], F32, 152)
        lvW = sb("lvW", [P, NT * HEADS, KL], F32, 160)
        lvP = sb("lvP", [P, NT * HEADS, KL], F32, 168)
        lw = sb("lw", [P, NT, P], BF16, 176)
        lsum = sb("lsum", [P, N], F32, 144)
        lind = sb("lind", [P, N], BF16, 160)
        acc6 = sb("acc6", [6, N], F32, 184)
        kr16 = sb("kr16", [6, N], I16, 144)
        den96 = sb("den96", [96, P], F32, 152)
        hn2 = sb("hn2", [P, NT * P], F32, 136)
        gw = sb("gw", [P, HEADS * P], F32, 168)
        hTc = [sb(f"hTc{i}", [P, P], F32, 170 + i) for i in range(2)]
        tf = [sb(f"tf{i}", [P, HEADS + 1, P], F32, 172 + 2 * i) for i in range(2)]
        tb = [sb(f"tb{i}", [P, HEADS + 1, 2, P], BF16, 176 + 2 * i) for i in range(2)]
        Ab = [sb(f"Ab{i}", [P, RB], F32, 32 + 4 * i) for i in range(2)]
        Ahi = [sb(f"Ahi{i}", [P, RB], BF16, 40 + 2 * i) for i in range(2)]
        Alo = [sb(f"Alo{i}", [P, RB], BF16, 44 + 2 * i) for i in range(2)]
        Tt = [sb(f"Tt{i}", [P, HEADS + 1, 2, P], BF16, 48 + 2 * i) for i in range(2)]
        tt = [sb(f"tt{i}", [P, HEADS, RB], FP16, 52 + 6 * i) for i in range(2)]
        ss = [sb(f"ss{i}", [P, HEADS, RB], BF16, 64 + 6 * i) for i in range(2)]
        ph = [sb(f"ph{i}", [P, HEADS, RB], BF16, 76 + 6 * i) for i in range(2)]
        pl = [sb(f"pl{i}", [P, HEADS, RB], BF16, 88 + 6 * i) for i in range(2)]
        KR = sb("KR", [P, HEADS, N], I16, 100)
        RD = sb("RD", [P, HEADS, RB], F32, 124)
        raw = sb("raw", [P, HEADS + 1, RB], F32, 136)
        esT = sb("esT", [P, N], F32, 152)
        nsT = sb("nsT", [P, N], F32, 168)
        dB = sb("dB", [P, N], F32, 184)
        gruW = sb("gruW", [P, 4, 3 * P], F32, 32)
        gruB = sb("gruB", [P, 4, 3], F32, 39)
        gbr = sb("gbr", [P, 2, 2], F32, 39.5)
        gR = [sb(f"gR{i}", [P, CH], F32, 40 + 2 * i) for i in range(2)]
        gZ = [sb(f"gZ{i}", [P, CH], F32, 44 + 2 * i) for i in range(2)]
        gM = [sb(f"gM{i}", [P, CH], F32, 48 + 2 * i) for i in range(2)]
        Wr = sb("Wr", [P, NE], F32, 56)
        rb2 = sb("rb2", [P, 2, NE], F32, 56.25)
        lg = sb("lg", [P, NT, NE], F32, 57)
        rq = sb("rq", [P, NT, NE], F32, 58)
        s1 = sb("s1", [P, NT, NE], F32, 59)
        s2 = sb("s2", [P, NT, NE], F32, 60)
        rs = sb("rs", [P, 8, NT], F32, 61)
        mk8 = sb("mk8", [NE, N], F32, 32)
        fW1 = sb("fW1", [P, 18 * KB // 4], F32, 64)
        fW2 = sb("fW2", [P, 18 * KB // 4], F32, 82)
        fB1 = sb("fB1", [P, 36], F32, 100)
        fB2 = sb("fB2", [P, 9], F32, 100.5)
        hid = [sb(f"hid{i}", [P, CH], F32, 101 + 2 * i) for i in range(12)]
        mB = sb("mB", [P, 2 * NE, CH], F32, 126)
        yT = [sb(f"yT{i}", [P, CH], F32, 158 + 2 * i) for i in range(2)]
        bw2f = sb("bw2f", [P, K1 * P], F32, 64)
        bw2 = [sb(f"bw2{i}", [P, K1 * P], BF16, 72 + 4 * i) for i in range(2)]
        bw1 = sb("bw1", [P, K1], F32, 80)
        bw1b = [sb(f"bw1b{i}", [P, K1], BF16, 80.25 + .25 * i) for i in range(2)]
        bw1T = sb("bw1T", [K1, P], F32, 81)
        bb = sb("bb", [K1, P], F32, 81.5)
        wb = sb("wb", [P, P], F32, 82)
        h3b = [sb(f"h3b{i}", [P, N], BF16, 84 + 8 * i) for i in range(2)]
        prod = [sb(f"prod{i}", [P, K1, P], F32, 100 + 8 * i) for i in range(2)]
        nodek = [sb(f"nodek{i}", [P, K1], F32, 116 + .25 * i) for i in range(2)]
        xf = [sb(f"xf{i}", [P, P], F32, 117 + .5 * i) for i in range(2)]
        Xb = [sb(f"Xb{i}", [P, NT, P], BF16, 48 + 8 * i) for i in range(2)]
        A4 = [sb(f"A4{i}", [P, N], F32, 128 + 16 * i) for i in range(2)]
        A4hi = [sb(f"A4hi{i}", [P, N], BF16, 160 + 8 * i) for i in range(2)]
        A4lo = [sb(f"A4lo{i}", [P, N], BF16, 176 + 8 * i) for i in range(2)]

        psum = ctx.enter_context(nc.psum_tensor("psum", [P, NC, CH], F32))
        flat = psum[:, :, :].rearrange("p b c -> p (b c)")

        hT_d, hn_d = dram("hT_d", [P, N], F32), dram("hn_d", [P, N], F32)
        diag_d = dram("diag_d", [N], F32)
        kr_d = dram("kr_d", [HEADS, N], I16)
        den_d, rden_d = dram("den_d", [HEADS, N], F32), dram("rden_d", [HEADS, N], F32)
        T_d = dram("T_d", [2 * NT * P, (HEADS + 1) * 2 * P], BF16)
        mk_d = [dram(f"mk_d{i}", [NE, N], F32) for i in range(2)]
        adj, adj_f = a["adjT"], a["adjT"].rearrange("a b -> (a b)")

        def S(*names):
            return [sem(n) for n in names]

        cst_in, x_in, gat_in, spilled, bf_consts = S("cst_in", "x_in", "gat_in", "spilled", "bf_consts")
        dve_steps, dve_lv, dve_ffn, dve_gru, dve_bil = S("dve_steps", "dve_lv", "dve_ffn", "dve_gru", "dve_bil")
        ln_turned, ln_centred, ln_squared, ln_var, ln_std, ln_normed, ln_back, ln_done = S(
            "ln_turned", "ln_centred", "ln_squared", "ln_var", "ln_std", "ln_normed", "ln_back", "ln_done")
        wa_ps, wa_ok, uv_ps, uv_ok = S("wa_ps", "wa_ok", "uv_ps", "uv_ok")
        m_in = S("m_in0", "m_in1")
        m_diag, m_mask, m_kept, m_neg, m_sum = S("m_diag", "m_mask", "m_kept", "m_neg", "m_sum")
        neg_rows, neg_tot, nsign_ok, x_sum, x_in2, x_mask, x_diag = S(
            "neg_rows", "neg_tot", "nsign_ok", "x_sum", "x_in2", "x_mask", "x_diag")
        top_l, top_g, far_l, far_g, groups_ok, frac_ok, wm_ok = S(
            "top_l", "top_g", "far_l", "far_g", "groups_ok", "frac_ok", "wm_ok")
        lv_cap, lv_exp, lv_w, lv_conv0, lv_conv1, lv_sum, lv_copied, lv_ind, lv_sel = S(
            "lv_cap", "lv_exp", "lv_w", "lv_conv0", "lv_conv1", "lv_sum", "lv_copied", "lv_ind", "lv_sel")
        ly_in, ly_mask, ly_sum, ly_diag, ly_w, ly_cap, ly_exp, lv_all, dve_ly = S(
            "ly_in", "ly_mask", "ly_sum", "ly_diag", "ly_w", "ly_cap", "ly_exp", "lv_all", "dve_ly")
        kr_ok, kr_out, den_out, den_back, rden_ok, rden_out, att_in, acc_done = S(
            "kr_ok", "kr_out", "den_out", "den_back", "rden_ok", "rden_out", "att_in", "acc_done")
        t_stage, t_ps, t_mul, t_slot3, t_hi, t_lo = S("t_stage", "t_ps", "t_mul", "t_slot3", "t_hi", "t_lo")
        tables_out, = S("tables_out")
        t_out = S("t_out0", "t_out1")
        a_in, at_in = S("a_in0", "a_in1"), S("at_in0", "at_in1")
        a_prep, a_relu, a_hi, a_lo, a_t, a_s, a_ph, a_pl, a_mm, a_fix = S(
            "a_prep", "a_relu", "a_hi", "a_lo", "a_t", "a_s", "a_ph", "a_pl", "a_mm", "a_fix")
        rd_in, raw_a, raw_d, comb = S("rd_in", "raw_a", "raw_d", "comb")
        gbr_ok, g_in, g_ps, g_gate, g_nin, g_tanh, g_used = S("gbr_ok", "g_in", "g_ps", "g_gate", "g_nin", "g_tanh", "g_used")
        r_in, r_ps, r_gap, r_exp, r_mask, r_tr, r_mk8, r_out = S(
            "r_in", "r_ps", "r_gap", "r_exp", "r_mask", "r_tr", "r_mk8", "r_out")
        up_done, act_done, down_done, y_used = [S(f"{n}_0", f"{n}_1") for n in
                                                ("up_done", "act_done", "down_done", "y_used")]
        mB_in = [S("mB_in00", "mB_in01"), S("mB_in10", "mB_in11")]
        b_in, b_hi, b_split, b_ps, b_node, b_prod, b_x, wb_ps, wb_ok = S(
            "b_in", "b_hi", "b_split", "b_ps", "b_node", "b_prod", "b_x", "wb_ps", "wb_ok")
        l_in = S("l_in0", "l_in1")
        l_hi, l_lo, l_mm, l_add = S("l_hi", "l_lo", "l_mm", "l_add")
        final, out_done = S("final", "out_done")

        def nlast(q):
            return ds(q * CH, CH)

        block = ctx.enter_context(nc.Block())

        @block.sync
        def _(sp):
            sp.dma_start(cst[:, :], a["consts"]).then_inc(cst_in, 16)
            sp.dma_start(xT[:, :], a["xT"]).then_inc(x_in, 16)
            sp.dma_start(gwTt[:, :], a["gatWT"]).then_inc(gat_in, 16)
            sp.dma_start(ga[:, :, :], a["gatA"]).then_inc(gat_in, 16)
            with nc.allow_non_contiguous_dma(reason="the diagonal of adj"):
                sp.dma_start(diag_d.rearrange("(a b) -> a b", a=16),
                             bass.AP(adj.tensor, 0, [[256 * (N + 1), 16], [N + 1, 256]])).then_inc(spilled, 16)
            sp.wait_ge(ln_done, 2)
            sp.dma_start(hT_d, hT[:, :]).then_inc(spilled, 16)
            sp.dma_start(hn_d, hn[:, :, :].rearrange("p t f -> p (t f)")).then_inc(spilled, 16)

            for s in range(2):
                sp.dma_start(Ar[s][:, :], adj[s * P:(s + 1) * P, :]).then_inc(m_in[s], 16)
            with sp.Fori(1, NT // 2) as i:
                for s in range(2):
                    sp.wait_ge(m_mask, 2 * i + s - 1)
                    sp.wait_ge(m_neg, 2 * i + s - 1)
                    sp.dma_start(Ar[s][:, :], adj[ds((2 * i + s) * P, P), :]).then_inc(m_in[s], 16)
            sp.wait_ge(nsign_ok, 1)
            nsign = sp.value_load(nsg[0:1, 0:1], min_val=1, max_val=2)
            with sp.If(nsign == 2):
                with sp.Fori(0, NT) as t:
                    sp.wait_ge(x_mask, t)
                    sp.dma_start(Ar[0][:, :], adj[ds(t * P, P), :]).then_inc(x_in2, 16)

            sp.wait_ge(groups_ok, 1)
            groups = sp.value_load(nsg[0:1, 1:2], min_val=1, max_val=1 << 20)
            with sp.If(nsign == 2):
                with sp.Fori(0, groups) as g:
                    with sp.Fori(0, NT) as t:
                        sp.wait_ge(ly_w, g + 1)
                        sp.wait_ge(ly_mask, g * NT + t)
                        sp.dma_start(Ar[0][:, :], adj[ds(t * P, P), :]).then_inc(ly_in, 16)

            sp.wait_ge(acc_done, 1)
            sp.dma_start(den_d, acc6[3:6, :]).then_inc(den_out, 16)
            sp.wait_ge(kr_ok, 1)
            sp.dma_start(kr_d, kr16[0:3, :]).then_inc(kr_out, 16)
            sp.wait_ge(den_out, 16)
            sp.dma_start(den96[:, :], den_d.rearrange("i (a b) -> (i a) b", b=P)).then_inc(den_back, 16)
            sp.dma_start(hT[:, :], hT_d).then_inc(att_in, 16)
            sp.dma_start(gw[:, :], a["gatW"]).then_inc(att_in, 16)
            sp.dma_start(xT[:, :], a["xT"]).then_inc(att_in, 16)
            sp.wait_ge(kr_out, 16)
            sp.dma_start(KR[:, :, :].rearrange("p i n -> p (i n)"),
                         kr_d.rearrange("i n -> (i n)").partition_broadcast(P)).then_inc(att_in, 16)
            sp.wait_ge(rden_ok, 1)
            sp.dma_start(rden_d.rearrange("i (a b) -> (i a) b", b=P), den96[:, :]).then_inc(rden_out, 16)
            sp.wait_ge(rden_out, 16)
            sp.wait_ge(kr_out, 16)
            sp.dma_start(hn2[:, :], hn_d).then_inc(att_in, 16)
            with sp.Fori(0, nsign) as sg:
                with sp.Fori(0, NT // 2) as i:
                    for s in range(2):
                        sp.wait_ge(t_lo, sg * NT + 2 * i + s + 2)
                        sp.dma_start(T_d[ds((sg * NT + 2 * i + s) * P, P), :],
                                     tb[s][:, :, :, :].rearrange("p h l f -> p (h l f)")).then_inc(t_out[s], 16)
            for s in range(2):
                sp.wait_ge(t_out[s], nsign * (16 * NT // 2))
                sp.sem_inc(tables_out, 1)

            with sp.Fori(0, NRB) as rb:
                sp.wait_ge(comb, rb * 5)
                for h in range(HEADS):
                    sp.dma_start(RD[:, h, :], rden_d[h:h + 1, ds(rb * RB, RB)]
                                 .rearrange("o n -> (o n)").partition_broadcast(P)).then_inc(rd_in, 16)
                with sp.Fori(0, nsign) as sg:
                    with sp.Fori(0, NT // 2) as i:
                        for s in range(2):
                            n = (rb * nsign + sg) * NT + 2 * i + s
                            sp.wait_ge(a_lo, n)
                            sp.dma_start(Ab[s][:, :], adj[ds((2 * i + s) * P, P), ds(rb * RB, RB)]
                                         ).then_inc(a_in[s], 16)
                            sp.wait_ge(a_mm, n)
                            sp.dma_start(Tt[s][:, :, :, :].rearrange("p h l f -> p (h l f)"),
                                         T_d[ds((sg * NT + 2 * i + s) * P, P), :]).then_inc(at_in[s], 16)

            sp.wait_ge(comb, NRB * 5)
            sp.dma_start(gruW[:, :, :], a["gruW"]).then_inc(g_in, 16)
            sp.dma_start(gruB[:, :, :], a["gruB"]).then_inc(g_in, 16)
            sp.dma_start(dB[:, :], diag_d.partition_broadcast(P)).then_inc(g_in, 16)

            def ffn_loads(k, nE, nF):
                sp.wait_ge(ln_done, 4 + 4 * k)
                for name, tile in (("Wr", Wr[:, :]), ("rb", rb2[:, :, :]),
                                   ("W1", fW1[:, 0:nE * nF * P]), ("W2", fW2[:, 0:nE * nF * P]),
                                   ("B1", fB1[:, 0:nE * nF]), ("B2", fB2[:, 0:nE])):
                    src = a[f"{name}_{k}"]
                    if name == "rb":
                        src = src.rearrange("a e -> (a e)").partition_broadcast(P)
                        tile = rb2[:, :, :].rearrange("p a e -> p (a e)")
                    sp.dma_start(tile, src).then_inc(r_in, 16)
                sp.wait_ge(r_mk8, k + 1)
                sp.dma_start(mk_d[k], mk8[:, :]).then_inc(r_out, 16)
                sp.wait_ge(r_out, 16 * (k + 1))
                first = nE - NE
                def weights(s, q):
                    for e in range(NE):
                        sp.dma_start(mB[:, NE * s + e, :], mk_d[k][e, ds(q * CH, CH)].partition_broadcast(P)
                                     ).then_inc(mB_in[k][s], 16)

                weights(0, 0)
                weights(1, 1)
                with sp.Fori(1, NC // 2) as i:
                    for s in range(2):
                        sp.wait_ge(y_used[k], (2 * i + s - 1) * nE + (3, 2)[k])
                        weights(s, 2 * i + s)

            ffn_loads(0, *FFN0)
            sp.wait_ge(ln_done, 6)
            sp.dma_start(bw2f[:, :], a["b_W2"]).then_inc(b_in, 16)
            sp.dma_start(bw1[:, :], a["b_W1"]).then_inc(b_in, 16)
            sp.dma_start(bw1T[:, :], a["b_W1T"]).then_inc(b_in, 16)
            sp.dma_start(bb[:, :], a["b_b"]).then_inc(b_in, 16)
            for s in range(2):
                sp.dma_start(A4[s][:, :], adj[s * P:(s + 1) * P, :]).then_inc(l_in[s], 16)
            with sp.Fori(1, NT // 2) as i:
                for s in range(2):
                    sp.wait_ge(l_lo, 2 * i + s - 1)
                    sp.dma_start(A4[s][:, :], adj[ds((2 * i + s) * P, P), :]).then_inc(l_in[s], 16)
            ffn_loads(1, *FFN1)
            sp.wait_ge(final, 1)
            sp.dma_start(out, xT[:, :]).then_inc(out_done, 16)
            sp.wait_ge(out_done, 16)
            sp.wait_ge(spilled, 48)

        @block.gpsimd
        def _(pool):
            pool.wait_ge(top_l, 1)
            pool.partition_all_reduce(sm[:, 3:6], sm[:, 0:3], P, ROP.max).then_inc(top_g, 1)
            pool.wait_ge(far_l, 1)
            pool.partition_all_reduce(sm[:, 7:8], sm[:, 6:7], P, ROP.max).then_inc(far_g, 1)
            pool.wait_ge(nsign_ok, 1)
            nsign = pool.value_load(nsg[0:1, 0:1], min_val=1, max_val=2)
            pool.sem_inc(a_lo, 1)
            for rb in range(NRB):
                with pool.Fori(0, nsign) as sg:
                    for lo, hi in ((0, rb * TPB), (rb * TPB, rb * TPB + TPB), (rb * TPB + TPB, NT)):
                        if lo == hi:
                            continue
                        diagonal = lo == rb * TPB
                        with pool.Fori(lo // 2, hi // 2) as i:
                            for s in range(2):
                                n = (rb * nsign + sg) * NT + 2 * i + s
                                pool.wait_ge(a_in[s], ((rb * nsign + sg) * (NT // 2) + i) * 16 + 16)
                                if diagonal:
                                    blk = Ab[s][:, ds((2 * i + s - rb * TPB) * P, P)]
                                    pool.tensor_tensor(blk, blk, offd, ALU.mult).then_inc(a_prep, 1)
                                else:
                                    pool.sem_inc(a_prep, 1)
                                pool.wait_ge(a_hi, n + 1)
                                pool.wait_ge(a_mm, n)
                                pool.tensor_tensor(Alo[s][:, :], Ab[s][:, :], Ahi[s][:, :], ALU.subtract
                                                   ).then_inc(a_lo, 1)

        def ln_scalar(act, k):
            for hf in range(2):
                act.wait_ge(ln_centred, 2 * k + hf + 1)
                if hf == 1:
                    act.wait_ge(ln_var, 2 * k + 1)
                nc.scalar.activation(sq[:, :, :], hn[:, 16 * hf:16 * hf + 16, :], ACT.Square).then_inc(ln_squared, 1)
                act.wait_ge(ln_var, 2 * k + hf + 1)
                nc.scalar.activation(stat[:, 3, 16 * hf:16 * hf + 16], stat[:, 2, 16 * hf:16 * hf + 16],
                                     ACT.Sqrt).then_inc(ln_std, 1)
            for hf in range(2):
                act.wait_ge(ln_back, 2 * k + hf + 1)
                nc.scalar.activation(hT[:, hf * N // 2:(hf + 1) * N // 2], flat[:, hf * N // 2:(hf + 1) * N // 2],
                                     ACT.Copy).then_inc(ln_done, 1)

        @block.scalar
        def _(act):
            ln_scalar(act, 0)
            with act.Fori(0, NT // 2) as i:
                for s in range(2):
                    act.wait_ge(m_diag, 2 * i + s + 1)
                    act.wait_ge(m_neg, 2 * i + s)
                    nc.scalar.activation(junk[:, :], Ar[s][:, :], ACT.Relu, scale=-1.0,
                                         accum_out=negs[:, ds(2 * i + s, 1)]).then_inc(m_neg, 1)
            act.wait_ge(nsign_ok, 1)
            nsign = act.value_load(nsg[0:1, 0:1], min_val=1, max_val=2)
            signed = act.value_load(nsg[0:1, 2:3], min_val=0, max_val=1)
            act.wait_ge(frac_ok, 1)
            nc.scalar.activation(wm[:, :], f6[:, :, :].rearrange("p s t -> p (s t)"), ACT.Exp).then_inc(wm_ok, 1)
            act.wait_ge(groups_ok, 1)
            groups = act.value_load(nsg[0:1, 1:2], min_val=1, max_val=1 << 20)
            with act.Fori(0, groups) as g:
                act.wait_ge(lv_cap, g + 1)
                nc.scalar.activation(lvE[:, :, :], lvE[:, :, :], ACT.Exp, scale=LEVEL * LN2).then_inc(lv_exp, 1)
                with act.Fori(0, NT // 2) as i:
                    act.wait_ge(lv_sum, g * NT + 2 * i)
                    nc.scalar.activation(Pb[1][:, :], keep[:, ds((2 * i + 1) * N, N)], ACT.Copy).then_inc(lv_conv1, 1)
                with act.If(nsign == 2):
                    act.wait_ge(ly_cap, g + 1)
                    nc.scalar.activation(lvE[:, :, :], lvE[:, :, :], ACT.Exp, scale=LEVEL * LN2).then_inc(ly_exp, 1)
                act.wait_ge(lv_all, g + 1)
                nc.scalar.activation(lsum[:, 0:N // 2], flat[:, 0:N // 2], ACT.Copy).then_inc(lv_copied, 1)

            act.wait_ge(att_in, 80)
            with act.Fori(0, nsign) as sg:
                with act.Fori(0, NT // 2) as i:
                    for s in range(2):
                        n = sg * NT + 2 * i + s
                        act.wait_ge(t_ps, n)
                        nc.scalar.activation(hTc[s][:, :], hT[:, ds((2 * i + s) * P, P)], ACT.Copy).then_inc(t_stage, 1)
                        act.wait_ge(t_lo, n)
                        nc.scalar.activation(tf[s][:, HEADS, :], hn2[:, ds((2 * i + s) * P, P)], ACT.Copy,
                                             scale=sgn[:, ds(sg, 1)]).then_inc(t_slot3, 1)
                        act.wait_ge(t_slot3, n + 1)
                        act.wait_ge(t_mul, n + 1)
                        act.wait_ge(t_out[s], (sg * (NT // 2) + i) * 16)
                        nc.scalar.activation(tb[s][:, :, 0, :], tf[s][:, :, :], ACT.Copy).then_inc(t_hi, 1)

            act.sem_inc(a_s, 1)
            with act.Fori(0, NRB) as rb:
                with act.Fori(0, nsign) as sg:
                    with act.Fori(0, NT // 2) as i:
                        for s in range(2):
                            n = (rb * nsign + sg) * NT + 2 * i + s
                            with act.If(nsign == 2):
                                act.wait_ge(a_prep, n + 1)
                                nc.scalar.activation(Ab[s][:, :], Ab[s][:, :], ACT.Relu,
                                                     scale=sgn[:, ds(sg, 1)]).then_inc(a_relu, 1)
                            act.wait_ge(a_relu, signed * (n + 1))
                            act.wait_ge(a_prep, n + 1)
                            act.wait_ge(a_mm, n)
                            nc.scalar.activation(Ahi[s][:, :], Ab[s][:, :], ACT.Copy).then_inc(a_hi, 1)
                            act.wait_ge(a_t, n + 1)
                            act.wait_ge(a_pl, n)
                            nc.scalar.activation(ss[s][:, :, :], tt[s][:, :, :], ACT.Exp,
                                                 scale=LEVEL * LN2).then_inc(a_s, 1)
                act.wait_ge(a_mm, (rb + 1) * nsign * NT + 1)
                act.wait_ge(comb, rb * 5)
                nc.scalar.activation(raw[:, 0:2, :].rearrange("p h r -> p (h r)"), flat[:, 0:2 * RB],
                                     ACT.Copy).then_inc(raw_a, 1)

            act.wait_ge(gbr_ok, 2)
            with act.Fori(0, NC) as q:
                for s in range(2):
                    n = 2 * q + s
                    act.wait_ge(g_ps, n + 1)
                    act.wait_ge(g_used, n)
                    nc.scalar.activation(gR[s][:, :], psum[:, 4 * s, :], ACT.Sigmoid,
                                         bias=gbr[:, s, 0:1]).then_inc(g_gate, 1)
                    nc.scalar.activation(gZ[s][:, :], psum[:, 4 * s + 1, :], ACT.Sigmoid,
                                         bias=gbr[:, s, 1:2]).then_inc(g_gate, 1)
                    act.wait_ge(g_nin, n + 1)
                    nc.scalar.activation(gM[s][:, :], gM[s][:, :], ACT.Tanh,
                                         bias=gruB[:, 2 * s, 2:3]).then_inc(g_tanh, 1)

            def ffn_scalar(k, nE, nF, func):
                ring, banks = (12, 8)[k], 4
                act.wait_ge(r_gap, k + 1)
                nc.scalar.activation(rs[:, 3, :], rs[:, 2, :], ACT.Exp).then_inc(r_exp, 1)
                act.wait_ge(r_tr, k + 1)
                nc.scalar.activation(mk8[:, :], flat[0:NE, :], ACT.Copy).then_inc(r_mk8, 1)
                act.sem_inc(act_done[k], banks)
                with act.Fori(0, NC) as q:
                    for e in range(nE):
                        act.wait_ge(down_done[k], q * nE + e + 1)
                        for f in range(nF):
                            j = e * nF + f
                            act.wait_ge(up_done[k], q * (nE * nF) + j + 1)
                            nc.scalar.activation(hid[j % ring][:, :], psum[:, j % banks, :], func,
                                                 bias=fB1[:, j:j + 1]).then_inc(act_done[k], 1)

            ln_scalar(act, 1)
            ffn_scalar(0, *FFN0, ACT.Gelu)
            ln_scalar(act, 2)
            act.wait_ge(b_in, 64)
            nc.scalar.activation(h3b[0][:, :], hT[:, :], ACT.Copy).then_inc(b_hi, 1)
            nc.scalar.activation(bw2[0][:, :], bw2f[:, :], ACT.Copy).then_inc(b_hi, 1)
            nc.scalar.activation(bw1b[0][:, :], bw1[:, :], ACT.Copy).then_inc(b_hi, 1)
            with act.Fori(0, NT // 2) as i:
                for s in range(2):
                    act.wait_ge(l_in[s], i * 16 + 16)
                    act.wait_ge(l_mm, 2 * i + s)
                    nc.scalar.activation(A4hi[s][:, :], A4[s][:, :], ACT.Copy).then_inc(l_hi, 1)
            ln_scalar(act, 3)
            ffn_scalar(1, *FFN1, ACT.Relu)

        def ln_tensor(pe, k):
            for hf in range(2):
                for t in range(16 * hf, 16 * hf + 16):
                    last = nc.tensor.transpose(flat[:, t * P:(t + 1) * P], xT[:, t * P:(t + 1) * P], ident)
                last.then_inc(ln_turned, 1)
            for hf in range(2):
                pe.wait_ge(ln_normed, 2 * k + hf + 1)
                for t in range(16 * hf, 16 * hf + 16):
                    last = nc.tensor.transpose(flat[:, t * P:(t + 1) * P], hn[:, t, :], ident)
                last.then_inc(ln_back, 1)

        @block.tensor
        def _(pe):
            pe.wait_ge(cst_in, 16)
            pe.wait_ge(x_in, 16)
            ln_tensor(pe, 0)
            pe.wait_ge(gat_in, 32)
            pe.wait_ge(ln_done, 2)
            for h in range(HEADS):
                last = nc.tensor.matmul(psum[:, 0, 2 * h:2 * h + 2], gwTt[:, h * P:(h + 1) * P], ga[:, h, :],
                                        start=(h == 0), stop=True, skip_group_check=True)
            last.then_inc(wa_ps, 1)
            pe.wait_ge(wa_ok, 1)
            for t in range(NT):
                last = nc.tensor.matmul(psum[:, 1, 6 * t:6 * t + 6], hT[:, t * P:(t + 1) * P],
                                        wa[:, :, :].rearrange("p a h -> p (a h)"),
                                        start=(t == 0), stop=True, skip_group_check=True)
            last.then_inc(uv_ps, 1)
            pe.wait_ge(uv_ok, 1)
            for b in range(2):
                nc.tensor.matmul(psum[:, b, 0:288], zero[:, 0:P], zero[:, 0:288], start=True, stop=False,
                                 skip_group_check=True)

            def sums(mask, uv, done):
                for t in range(NT):
                    last = nc.tensor.matmul(psum[:, t // 16, 18 * (t % 16):18 * (t % 16) + 18],
                                            mask[:, t * P:(t + 1) * P], uv,
                                            start=False, stop=False, skip_group_check=True)
                last.then_inc(done, 1)

            pe.sem_inc(m_sum, 1)
            with pe.Fori(0, NT // 2) as i:
                for s in range(2):
                    pe.wait_ge(m_mask, 2 * i + s + 1)
                    sums(Pb[s], uvs[:, ds(2 * i + s, 1), :, :].rearrange("p o a b -> p (o a b)"), m_sum)
            pe.wait_ge(neg_rows, 1)
            nc.tensor.matmul(psum[:, 2, 0:1], ones, sm[:, 9:10], start=True, stop=True).then_inc(neg_tot, 1)
            pe.wait_ge(nsign_ok, 1)
            nsign = pe.value_load(nsg[0:1, 0:1], min_val=1, max_val=2)
            with pe.If(nsign == 2):
                with pe.Fori(0, NT) as t:
                    pe.wait_ge(x_mask, t + 1)
                    sums(Pb[0], uvx[:, ds(t, 1), :, :].rearrange("p o a b -> p (o a b)"), x_sum)

            pe.wait_ge(groups_ok, 1)
            groups = pe.value_load(nsg[0:1, 1:2], min_val=1, max_val=1 << 20)

            def levels(mask, t, done):
                for q in range(NC):
                    last = nc.tensor.matmul(psum[:, q, :], lw[:, ds(t, 1), :].rearrange("p o c -> p (o c)"),
                                            mask[:, q * CH:(q + 1) * CH], start=False, stop=False,
                                            skip_group_check=True)
                last.then_inc(done, 1)

            with pe.Fori(0, groups) as g:
                pe.wait_ge(lv_w, g + 1)
                pe.wait_ge(lv_ind, 3 * g)
                for q in range(NC):
                    nc.tensor.matmul(psum[:, q, :], zero[:, 0:P], zero[:, :], start=True, stop=False,
                                     skip_group_check=True)
                with pe.Fori(0, NT // 2) as i:
                    pe.wait_ge(lv_conv0, g * (NT // 2) + i + 1)
                    levels(Pb[0], 2 * i, lv_sum)
                    pe.wait_ge(lv_conv1, g * (NT // 2) + i + 1)
                    levels(Pb[1], 2 * i + 1, lv_sum)
                with pe.If(nsign == 2):
                    with pe.Fori(0, NT) as t:
                        pe.wait_ge(ly_mask, g * NT + t + 1)
                        levels(Pb[0], t, ly_sum)
                nc.tensor.matmul(psum[:, 0, 0:1], zero[:, 0:P], zero[:, 0:1], start=False, stop=False,
                                 skip_group_check=True).then_inc(lv_all, 1)
                pe.wait_ge(lv_ind, 3 * g + 2)
                pe.wait_ge(lv_copied, g + 1)
                for q in range(NC):
                    nc.tensor.matmul(psum[0:6, q, :], selC[:, :], lind[:, q * CH:(q + 1) * CH], start=True,
                                     stop=False)
                    last = nc.tensor.matmul(psum[0:6, q, :], selD, lsum[:, q * CH:(q + 1) * CH], start=False,
                                            stop=True)
                last.then_inc(lv_sel, 1)

            pe.wait_ge(acc_done, 1)
            pe.sem_inc(t_ps, 1)
            with pe.Fori(0, nsign) as sg:
                with pe.Fori(0, NT // 2) as i:
                    for s in range(2):
                        n = sg * NT + 2 * i + s
                        pe.wait_ge(t_stage, n + 1)
                        pe.wait_ge(t_lo, n)
                        nc.tensor.matmul(psum[:, s, 0:HEADS * P], hTc[s][:, :], gw[:, :], start=True,
                                         stop=True).then_inc(t_ps, 1)

            pe.sem_inc(a_mm, 1)
            with pe.Fori(0, NRB) as rb:
                pe.wait_ge(raw_a, rb)
                pe.wait_ge(raw_d, rb)
                pe.wait_ge(t_lo, nsign * NT + 1)
                for q in range(NC):
                    nc.tensor.matmul(psum[:, q, :], zero[:, 0:P], zero[:, :], start=True, stop=False,
                                     skip_group_check=True)
                with pe.Fori(0, nsign) as sg:
                    with pe.Fori(0, NT // 2) as i:
                        for s in range(2):
                            m = (rb * nsign + sg) * (NT // 2) + i
                            n = (rb * nsign + sg) * NT + 2 * i + s
                            pe.wait_ge(at_in[s], m * 16 + 16)
                            pe.wait_ge(a_hi, n + 1)
                            pe.wait_ge(a_lo, n + 2)
                            for h in (HEADS, 0, 1, 2):
                                if h == 0:
                                    pe.wait_ge(a_ph, n + 1)
                                    pe.wait_ge(a_pl, n + 2)
                                hi = Ahi[s][:, :] if h == HEADS else ph[s][:, h, :]
                                lo = Alo[s][:, :] if h == HEADS else pl[s][:, h, :]
                                for w, mv in ((0, hi), (0, lo), (1, hi)):
                                    for q in range(RB // CH):
                                        last = nc.tensor.matmul(psum[:, 2 * h + q, :], Tt[s][:, h, w, :],
                                                                mv[:, q * CH:(q + 1) * CH], start=False,
                                                                stop=False, skip_group_check=True)
                            last.then_inc(a_mm, 1)

            pe.wait_ge(g_in, 48)
            pe.wait_ge(comb, NRB * 5)
            with pe.Fori(0, NC) as q:
                for s in range(2):
                    src = (nsT, esT)[s][:, nlast(q)]
                    hh = hT[:, nlast(q)]
                    pe.wait_ge(g_used, 2 * q + s)
                    for g in range(2):
                        nc.tensor.matmul(psum[:, 4 * s + g, :], gruW[:, 2 * s, g * P:(g + 1) * P], src,
                                         start=True, stop=False)
                        nc.tensor.matmul(psum[:, 4 * s + g, :], gruW[:, 2 * s + 1, g * P:(g + 1) * P], hh,
                                         start=False, stop=True)
                    nc.tensor.matmul(psum[:, 4 * s + 2, :], gruW[:, 2 * s, 2 * P:], src, start=True, stop=True)
                    nc.tensor.matmul(psum[:, 4 * s + 3, :], gruW[:, 2 * s + 1, 2 * P:], hh, start=True,
                                     stop=True).then_inc(g_ps, 1)

            def ffn_tensor(k, nE, nF):
                ring, banks, dn = (12, 8)[k], 4, (3, 2)[k]
                pe.wait_ge(r_in, 96 * (k + 1))
                pe.wait_ge(ln_done, 4 + 4 * k)
                for t in range(NT):
                    last = nc.tensor.matmul(psum[:, 0, NE * t:NE * t + NE], hT[:, t * P:(t + 1) * P], Wr[:, :],
                                            start=(t == 0), stop=True, skip_group_check=True)
                last.then_inc(r_ps, 1)
                pe.wait_ge(r_mask, k + 1)
                for t in range(NT):
                    last = nc.tensor.transpose(flat[0:NE, t * P:(t + 1) * P], s1[:, t, :], ident)
                last.then_inc(r_tr, 1)
                pe.wait_ge(r_mk8, k + 1)
                pe.sem_inc(down_done[k], ring // nF)
                with pe.Fori(0, NC) as q:
                    def down(e):
                        pe.wait_ge(act_done[k], q * (nE * nF) + banks + (e + 1) * nF)
                        pe.wait_ge(y_used[k], q * nE + e + 1)
                        for f in range(nF):
                            j = e * nF + f
                            last = nc.tensor.matmul(psum[:, banks + e % dn, :], fW2[:, j * P:(j + 1) * P],
                                                    hid[j % ring][:, :], start=(f == 0), stop=(f == nF - 1))
                        last.then_inc(down_done[k], 1)

                    for e in range(nE):
                        for f in range(nF):
                            j = e * nF + f
                            pe.wait_ge(act_done[k], q * (nE * nF) + j + 1)
                            nc.tensor.matmul(psum[:, j % banks, :], fW1[:, j * P:(j + 1) * P], hT[:, nlast(q)],
                                             start=True, stop=True).then_inc(up_done[k], 1)
                        if e:
                            down(e - 1)
                    down(nE - 1)

            pe.wait_ge(g_used, 2 * NC + 1)
            ln_tensor(pe, 1)
            ffn_tensor(0, *FFN0)
            pe.wait_ge(y_used[0], NC * FFN0[0] + 3)
            pe.wait_ge(dve_ffn, NC * (2 * NE + 1))
            ln_tensor(pe, 2)
            pe.wait_ge(b_split, 1)
            pe.wait_ge(ln_done, 6)
            with pe.Fori(0, NT // 2) as i:
                for s in range(2):
                    n = 2 * i + s
                    pe.wait_ge(b_prod, n)
                    for w, (x, y) in enumerate(((0, 0), (0, 1), (1, 0))):
                        last = nc.tensor.matmul(psum[:, 4 * s, 0:K1], h3b[x][:, ds(n * P, P)], bw1b[y][:, :],
                                                start=(w == 0), stop=(w == 2))
                    last.then_inc(b_node, 1)
                    pe.wait_ge(b_x, 3 * n + 1)
                    for c in range(4):
                        for w, (x, y) in enumerate(((0, 0), (0, 1), (1, 0))):
                            last = nc.tensor.matmul(psum[:, 4 * s + c, :], h3b[x][:, ds(n * P, P)],
                                                    bw2[y][:, c * CH:(c + 1) * CH], start=(w == 0),
                                                    stop=(w == 2))
                    last.then_inc(b_ps, 1)
            pe.wait_ge(b_prod, NT + 1)
            pe.wait_ge(b_in, 64)
            nc.tensor.matmul(psum[:, 0, 0:P], bw1T[:, :], bb[:, :], start=True, stop=True).then_inc(wb_ps, 1)
            pe.wait_ge(wb_ok, 1)
            for q in range(NC):
                nc.tensor.matmul(psum[:, q, :], wb[:, :], hT[:, q * CH:(q + 1) * CH], start=True, stop=False,
                                 skip_group_check=True)
            pe.wait_ge(b_x, 3 * NT)
            pe.sem_inc(l_mm, 1)
            with pe.Fori(0, NT // 2) as i:
                for s in range(2):
                    n = 2 * i + s
                    pe.wait_ge(l_hi, n + 1)
                    pe.wait_ge(l_lo, n + 1)
                    for w, mv in ((0, A4hi), (0, A4lo), (1, A4hi)):
                        for q in range(NC):
                            last = nc.tensor.matmul(psum[:, q, :], Xb[w][:, ds(n, 1), :].rearrange("p o f -> p (o f)"),
                                                    mv[s][:, q * CH:(q + 1) * CH], start=False, stop=False,
                                                    skip_group_check=True)
                    last.then_inc(l_mm, 1)
            pe.wait_ge(l_add, NC)
            ln_tensor(pe, 3)
            ffn_tensor(1, *FFN1)

        @block.vector
        def _(dve):
            V = nc.vector
            c = Chain(dve, dve_steps)

            def ln_vector(k):
                for hf in range(2):
                    t = slice(16 * hf, 16 * hf + 16)
                    ps = flat[:, hf * N // 2:(hf + 1) * N // 2].rearrange("p (t f) -> p t f", f=P)
                    wide = [P, 16, P]
                    dve.wait_ge(ln_turned, 2 * k + hf + 1)
                    c.link(V.tensor_reduce(stat[:, 0, t], ps, AX, ALU.add))
                    c.link(V.tensor_scalar(stat[:, 1, t], stat[:, 0, t], 1.0 / P, None, ALU.mult))
                    V.tensor_tensor(hn[:, t, :], ps, stat[:, 1, t].unsqueeze(2).to_broadcast(wide),
                                    ALU.subtract).then_inc(ln_centred, 1)
                for hf in range(2):
                    t = slice(16 * hf, 16 * hf + 16)
                    dve.wait_ge(ln_squared, 2 * k + hf + 1)
                    c.link(V.tensor_reduce(stat[:, 0, t], sq[:, :, :], AX, ALU.add))
                    V.tensor_scalar(stat[:, 2, t], stat[:, 0, t], 1.0 / P, EPS, ALU.mult, ALU.add).then_inc(ln_var, 1)
                    dve.wait_ge(ln_std, 2 * k + hf + 1)
                    dve.wait_ge(ln_var, 2 * k + hf + 1)
                    dve.wait_ge(ln_centred, 2 * k + hf + 1)
                    c.link(V.reciprocal(stat[:, 4, t], stat[:, 3, t]))
                    c.link(V.tensor_tensor(stat[:, 5, t], stat[:, 4, t], stat[:, 4, t], ALU.mult))
                    c.link(V.tensor_tensor(stat[:, 5, t], stat[:, 5, t], stat[:, 2, t], ALU.mult))
                    c.link(V.tensor_scalar(stat[:, 5, t], stat[:, 5, t], -0.5, 1.5, ALU.mult, ALU.add))
                    c.link(V.tensor_tensor(stat[:, 4, t], stat[:, 4, t], stat[:, 5, t], ALU.mult))
                    V.tensor_tensor(hn[:, t, :], hn[:, t, :], stat[:, 4, t].unsqueeze(2).to_broadcast([P, 16, P]),
                                    ALU.mult).then_inc(ln_normed, 1)

            dve.wait_ge(cst_in, 16)
            c.link(V.memset(zero[:, :], 0.0))
            c.link(V.tensor_copy(selC[:, :], selCf))
            ln_vector(0)
            dve.wait_ge(wa_ps, 1)
            V.tensor_copy(wa[:, :, :], psum[:, 0, 0:6].rearrange("p (h a) -> p a h", a=2)).then_inc(wa_ok, 1)
            dve.wait_ge(uv_ps, 1)
            ps = psum[:, 1, 0:6 * NT].rearrange("p (t x) -> p t x", x=6)
            c.link(V.tensor_copy(uvs[:, :, 0, :], ps))
            c.link(V.tensor_tensor(uvr[:, :, :], ps, uvs[:, :, 0, :], ALU.subtract))
            c.link(V.tensor_copy(uvs[:, :, 1, :], uvr[:, :, :]))
            c.link(V.tensor_tensor(uvr[:, :, :], uvr[:, :, :], uvs[:, :, 1, :], ALU.subtract))
            c.link(V.tensor_copy(uvs[:, :, 2, :], uvr[:, :, :]))
            for part in range(3):
                c.link(V.tensor_copy(uvx[:, :, part, 0:3], uvs[:, :, part, 3:6]))
                c.link(V.tensor_copy(uvx[:, :, part, 3:6], uvs[:, :, part, 0:3]))
            V.memset(sm[:, :], 0.0).then_inc(uv_ok, 1)
            dve.wait_ge(uv_ok, 1)
            dve.wait_ge(spilled, 48)

            with dve.Fori(0, NT // 2) as i:
                for s in range(2):
                    n = 2 * i + s
                    blk = Ar[s][:, ds(n * P, P)]
                    dve.wait_ge(m_in[s], i * 16 + 16)
                    V.tensor_tensor(blk, blk, offd, ALU.mult).then_inc(m_diag, 1)
                    dve.wait_ge(m_diag, n + 1)
                    dve.wait_ge(m_sum, n)
                    V.tensor_scalar(Pb[s][:, :], Ar[s][:, :], 0.0, None, ALU.is_gt).then_inc(m_mask, 1)
                    dve.wait_ge(m_mask, n + 1)
                    V.tensor_copy(keep[:, ds(n * N, N)], Pb[s][:, :]).then_inc(m_kept, 1)
            dve.wait_ge(m_neg, NT)
            V.tensor_reduce(sm[:, 9:10], negs[:, :], AX, ALU.add).then_inc(neg_rows, 1)
            dve.wait_ge(neg_tot, 1)
            c.link(V.tensor_scalar(sm[:, 10:11], psum[:, 2, 0:1], 0.0, None, ALU.is_gt))
            c.link(V.tensor_scalar(sm[:, 11:12], sm[:, 10:11], 1.0, None, ALU.add))
            c.link(V.tensor_scalar(sm[:, 12:13], sm[:, 10:11], -1.0, 1.0, ALU.mult, ALU.add))
            c.link(V.tensor_copy(nsg[:, 2:3], sm[:, 10:11]))
            V.tensor_copy(nsg[:, 0:1], sm[:, 11:12]).then_inc(nsign_ok, 1)
            dve.wait_ge(nsign_ok, 1)
            nsign = dve.value_load(nsg[0:1, 0:1], min_val=1, max_val=2)
            dve.wait_ge(m_kept, NT)
            with dve.If(nsign == 2):
                with dve.Fori(0, NT) as t:
                    blk = Ar[0][:, ds(t * P, P)]
                    dve.wait_ge(x_in2, t * 16 + 16)
                    V.tensor_tensor(blk, blk, offd, ALU.mult).then_inc(x_diag, 1)
                    dve.wait_ge(x_diag, t + 1)
                    dve.wait_ge(x_sum, t)
                    V.tensor_scalar(Pb[0][:, :], Ar[0][:, :], 0.0, None, ALU.is_lt).then_inc(x_mask, 1)
                dve.wait_ge(x_sum, NT)
            dve.wait_ge(m_sum, NT + 1)
            c.link(V.tensor_copy(zs[:, 0:16, :], psum[:, 0, 0:288].rearrange("p (t x) -> p t x", x=18)))
            c.link(V.tensor_copy(zs[:, 16:32, :], psum[:, 1, 0:288].rearrange("p (t x) -> p t x", x=18)))
            c.link(V.tensor_tensor(z6[:, :, :], zs[:, :, 12:18], zs[:, :, 6:12], ALU.add))
            c.link(V.tensor_tensor(z6[:, :, :], z6[:, :, :], zs[:, :, 0:6], ALU.add))
            z4 = z6[:, :, :].rearrange("p t (s h) -> p t s h", s=2)
            for sg in range(2):
                e3 = e6[:, sg, :].rearrange("p (t h) -> p t h", h=HEADS)
                c.link(V.scalar_tensor_tensor(out=e3, in0=z4[:, :, sg, :], scalar=SLOPE, in1=z4[:, :, sg, :],
                                              op0=ALU.mult, op1=ALU.max))
            c.link(V.tensor_scalar(f6[:, 0, :], e6[:, 0, :], sm[:, 12:13], None, ALU.mult))
            c.link(V.scalar_tensor_tensor(out=e6[:, 1, :], in0=e6[:, 1, :], scalar=sm[:, 10:11], in1=f6[:, 0, :],
                                          op0=ALU.mult, op1=ALU.add))
            c.link(V.tensor_scalar(q6[:, :, :], e6[:, :, :], 1.0 / LN2, None, ALU.mult))
            c.link(V.tensor_scalar(q6[:, :, :], q6[:, :, :], ROUND, None, ALU.add))
            c.link(V.tensor_scalar(q6[:, :, :], q6[:, :, :], -ROUND, None, ALU.add))
            c.link(V.scalar_tensor_tensor(out=f6[:, :, :], in0=q6[:, :, :], scalar=-LN2_HI, in1=e6[:, :, :],
                                          op0=ALU.mult, op1=ALU.add))
            V.scalar_tensor_tensor(out=f6[:, :, :], in0=q6[:, :, :], scalar=-LN2_LO, in1=f6[:, :, :],
                                   op0=ALU.mult, op1=ALU.add).then_inc(frac_ok, 1)
            V.tensor_reduce(sm[:, 0:3], q6[:, :, :].rearrange("p s (t h) -> p h (s t)", h=HEADS), AX,
                            ALU.max).then_inc(top_l, 1)
            dve.wait_ge(top_g, 1)
            for sg in range(2):
                d3 = dpt[:, sg * NT * HEADS:(sg + 1) * NT * HEADS].rearrange("p (t h) -> p t h", h=HEADS)
                c.link(V.tensor_tensor(d3, q6[:, sg, :].rearrange("p (t h) -> p t h", h=HEADS),
                                       sm[:, 3:6].unsqueeze(1).to_broadcast([P, NT, HEADS]), ALU.subtract))
            c.link(V.tensor_scalar(dpt[:, :], dpt[:, :], 1.0 / LEVEL, None, ALU.mult))
            c.link(V.tensor_reduce(sm[:, 8:9], dpt[:, :], AX, ALU.min))
            V.tensor_scalar(sm[:, 6:7], sm[:, 8:9], -1.0, None, ALU.mult).then_inc(far_l, 1)
            dve.wait_ge(far_g, 1)
            c.link(V.tensor_scalar(sm[:, 13:14], sm[:, 7:8], 1.0 / KL, 0.51, ALU.mult, ALU.add))
            c.link(V.tensor_scalar(sm[:, 13:14], sm[:, 13:14], 1.0, None, ALU.max))
            c.link(V.tensor_copy(lev[:, :], kk))
            c.link(V.memset(acc6[:, :], 0.0))
            c.link(V.memset(lw[:, :, 2 * PART:P], 0.0))
            V.tensor_copy(nsg[:, 1:2], sm[:, 13:14]).then_inc(groups_ok, 1)
            dve.wait_ge(groups_ok, 1)
            dve.wait_ge(wm_ok, 1)
            groups = dve.value_load(nsg[0:1, 1:2], min_val=1, max_val=1 << 20)

            LVSTEPS = 8

            def level_weights(l, sg, cap, exp, nexp, last):
                dp = dpt[:, sg * NT * HEADS:(sg + 1) * NT * HEADS].unsqueeze(2).to_broadcast([P, NT * HEADS, KL])
                w = wm[:, sg * NT * HEADS:(sg + 1) * NT * HEADS].unsqueeze(2).to_broadcast([P, NT * HEADS, KL])
                lb = lev[:, :].unsqueeze(1).to_broadcast([P, NT * HEADS, KL])
                l.link(V.tensor_tensor(lvU[:, :, :], dp, lb, ALU.add))
                V.tensor_scalar(lvE[:, :, :], lvU[:, :, :], 0.0, None, ALU.min).then_inc(cap, 1)
                l.link(V.tensor_scalar(lvP[:, :, :], lvU[:, :, :], 0.0, POISON, ALU.is_gt, ALU.mult))
                dve.wait_ge(exp, nexp)
                l.link(V.tensor_tensor(lvW[:, :, :], lvE[:, :, :], w, ALU.mult))
                l.link(V.tensor_tensor(lvW[:, :, :], lvW[:, :, :], lvP[:, :, :], ALU.add))
                W = lvW[:, :, :].rearrange("p (t h) k -> p t (h k)", h=HEADS)
                U = lvU[:, :, :].rearrange("p (t h) k -> p t (h k)", h=HEADS)
                PZ = lvP[:, :, :].rearrange("p (t h) k -> p t (h k)", h=HEADS)
                l.link(V.tensor_copy(lw[:, :, 0:PART], W))
                l.link(V.tensor_tensor(U, W, lw[:, :, 0:PART], ALU.subtract))
                V.tensor_tensor(lw[:, :, PART:2 * PART], U, PZ, ALU.add).then_inc(last, 1)

            with dve.Fori(0, groups) as g:
                l = Chain(dve, dve_lv, g * LVSTEPS)
                level_weights(l, 0, lv_cap, lv_exp, g + 1, lv_w)
                with dve.Fori(0, NT // 2) as i:
                    dve.wait_ge(lv_sum, g * NT + 2 * i)
                    V.tensor_copy(Pb[0][:, :], keep[:, ds((2 * i) * N, N)]).then_inc(lv_conv0, 1)
                with dve.If(nsign == 2):
                    dve.wait_ge(lv_sum, (g + 1) * NT)
                    level_weights(Chain(dve, dve_ly, g * 6), 1, ly_cap, ly_exp, g + 1, ly_w)
                    with dve.Fori(0, NT) as t:
                        blk = Ar[0][:, ds(t * P, P)]
                        dve.wait_ge(ly_in, (g * NT + t) * 16 + 16)
                        V.tensor_tensor(blk, blk, offd, ALU.mult).then_inc(ly_diag, 1)
                        dve.wait_ge(ly_diag, g * NT + t + 1)
                        dve.wait_ge(ly_sum, g * NT + t)
                        V.tensor_scalar(Pb[0][:, :], Ar[0][:, :], 0.0, None, ALU.is_lt).then_inc(ly_mask, 1)
                dve.wait_ge(lv_all, g + 1)
                l.link(V.tensor_copy(lsum[:, N // 2:], flat[:, N // 2:]))
                l.link(V.tensor_scalar(lev[:, :], lev[:, :], float(KL), None, ALU.add))
                dve.wait_ge(lv_copied, g + 1)
                V.tensor_scalar(lind[:, :], lsum[:, :], CLEAN, None, ALU.is_lt).then_inc(lv_ind, 1)
                V.scalar_tensor_tensor(out=lsum[:, :], in0=lsum[:, :], scalar=CLEAN, in1=lsum[:, :],
                                       op0=ALU.is_lt, op1=ALU.mult).then_inc(lv_ind, 1)
                dve.wait_ge(lv_sel, g + 1)
                V.tensor_tensor(acc6[:, :], acc6[:, :], flat[0:6, :], ALU.add).then_inc(lv_ind, 1)
                dve.wait_ge(lv_ind, 3 * g + 3)
                assert l.n == LVSTEPS, l.n
            V.tensor_scalar(kr16[:, :], acc6[:, :], -1.0, 30000.0, ALU.add, ALU.min).then_inc(kr_ok, 1)
            V.tensor_copy(sm[:, 15:16], sm[:, 10:11]).then_inc(acc_done, 1)
            dve.wait_ge(den_back, 16)
            c.link(V.tensor_scalar(den96[:, :], den96[:, :], TINY, None, ALU.max))
            c.link(V.reciprocal(den96[:, :], den96[:, :]))
            V.tensor_scalar(den96[:, :], den96[:, :], 1.0 / HEADS, None, ALU.mult).then_inc(rden_ok, 1)

            dve.wait_ge(att_in, 80)
            dve.sem_inc(t_lo, 1)
            with dve.Fori(0, nsign) as sg:
                with dve.Fori(0, NT // 2) as i:
                    for s in range(2):
                        n = sg * NT + 2 * i + s
                        dve.wait_ge(t_ps, n + 2)
                        V.scalar_tensor_tensor(
                            out=tf[s][:, 0:HEADS, :], in0=psum[:, s, 0:HEADS * P].rearrange("p (h f) -> p h f", f=P),
                            scalar=sgn[:, ds(sg, 1)],
                            in1=wm[:, ds(n * HEADS, HEADS)].unsqueeze(2).to_broadcast([P, HEADS, P]),
                            op0=ALU.mult, op1=ALU.mult).then_inc(t_mul, 1)
                        dve.wait_ge(t_mul, n + 1)
                        dve.wait_ge(t_hi, n + 1)
                        V.tensor_tensor(tb[s][:, :, 1, :], tf[s][:, :, :], tb[s][:, :, 0, :],
                                        ALU.subtract).then_inc(t_lo, 1)

            dve.sem_inc(a_pl, 1)
            with dve.Fori(0, NRB) as rb:
                def scale(sg, t, s, n):
                    dve.wait_ge(a_s, n)
                    for h in range(HEADS):
                        last = V.tensor_scalar(tt[s][:, h, :], KR[:, h, ds(rb * RB, RB)],
                                               dpt[:, ds((sg * NT + t) * HEADS + h, 1)], 0.0, ALU.add, ALU.min)
                    last.then_inc(a_t, 1)

                def parts(s, n):
                    dve.wait_ge(a_s, n + 2)
                    dve.wait_ge(a_hi, n + 1)
                    dve.wait_ge(a_mm, n)
                    V.tensor_tensor(ph[s][:, :, :], ss[s][:, :, :],
                                    Ahi[s][:, :].unsqueeze(1).to_broadcast([P, HEADS, RB]), ALU.mult).then_inc(a_ph, 1)
                    dve.wait_ge(a_lo, n + 2)
                    V.tensor_tensor(pl[s][:, :, :], ss[s][:, :, :],
                                    Alo[s][:, :].unsqueeze(1).to_broadcast([P, HEADS, RB]), ALU.mult).then_inc(a_pl, 1)

                with dve.Fori(0, nsign) as sg:
                    n0 = (rb * nsign + sg) * NT
                    scale(sg, 0, 0, n0)
                    with dve.Fori(0, NT // 2 - 1) as i:
                        for s in range(2):
                            scale(sg, 2 * i + s + 1, 1 - s, n0 + 2 * i + s + 1)
                            parts(s, n0 + 2 * i + s)
                    scale(sg, NT - 1, 1, n0 + (NT - 1))
                    parts(0, n0 + (NT - 2))
                    parts(1, n0 + (NT - 1))
                dve.wait_ge(a_mm, (rb + 1) * nsign * NT + 1)
                V.tensor_copy(raw[:, 2:4, :].rearrange("p h r -> p (h r)"), flat[:, 2 * RB:]).then_inc(raw_d, 1)
                dve.wait_ge(rd_in, rb * 48 + 48)
                dve.wait_ge(raw_a, rb + 1)
                dve.wait_ge(raw_d, rb + 1)
                V.tensor_tensor(raw[:, 0:HEADS, :], raw[:, 0:HEADS, :], RD[:, :, :], ALU.mult).then_inc(comb, 1)
                V.tensor_copy(nsT[:, ds(rb * RB, RB)], raw[:, HEADS, :]).then_inc(comb, 1)
                dve.wait_ge(comb, rb * 5 + 1)
                V.tensor_tensor(raw[:, 0, :], raw[:, 0, :], raw[:, 1, :], ALU.add).then_inc(comb, 1)
                dve.wait_ge(comb, rb * 5 + 3)
                V.tensor_tensor(esT[:, ds(rb * RB, RB)], raw[:, 0, :], raw[:, 2, :], ALU.add).then_inc(comb, 1)
                V.tensor_copy(sm[:, 15:16], sm[:, 10:11]).then_inc(comb, 1)
                dve.wait_ge(comb, rb * 5 + 5)

            dve.wait_ge(g_in, 48)
            for s in range(2):
                V.tensor_tensor(gbr[:, s, :], gruB[:, 2 * s, 0:2], gruB[:, 2 * s + 1, 0:2],
                                ALU.add).then_inc(gbr_ok, 1)
            dve.sem_inc(g_used, 1)
            with dve.Fori(0, NC) as q:
                gc = Chain(dve, dve_gru, q * 12)
                for s in range(2):
                    n = 2 * q + s
                    dve.wait_ge(g_gate, n * 2 + 2)
                    gc.link(V.scalar_tensor_tensor(out=gM[s][:, :], in0=psum[:, 4 * s + 3, :],
                                                   scalar=gruB[:, 2 * s + 1, 2:3], in1=gR[s][:, :], op0=ALU.add,
                                                   op1=ALU.mult))
                    V.tensor_tensor(gM[s][:, :], gM[s][:, :], psum[:, 4 * s + 2, :], ALU.add).then_inc(g_nin, 1)
                    dve.wait_ge(g_tanh, n + 1)
                    gc.link(V.tensor_tensor(gR[s][:, :], hT[:, nlast(q)], gM[s][:, :], ALU.subtract))
                    gc.link(V.tensor_tensor(gR[s][:, :], gR[s][:, :], gZ[s][:, :], ALU.mult))
                    gc.link(V.tensor_tensor(gR[s][:, :], gR[s][:, :], gM[s][:, :], ALU.add))
                    gc.link(V.tensor_tensor(gR[s][:, :], gR[s][:, :], dB[:, nlast(q)], ALU.mult))
                    gc.link(V.tensor_tensor(xT[:, nlast(q)], xT[:, nlast(q)], gR[s][:, :], ALU.add))
                    dve.sem_inc(g_used, 1)
                assert gc.n == 12, gc.n

            def ffn_vector(k, nE):
                dn = (3, 2)[k]
                T = [P, NT, NE]
                dve.wait_ge(r_ps, k + 1)
                ps = psum[:, 0, 0:NT * NE].rearrange("p (t e) -> p t e", e=NE)
                c.link(V.tensor_tensor(lg[:, :, :], ps, rb2[:, 0, :].unsqueeze(1).to_broadcast(T), ALU.add))
                c.link(V.tensor_tensor(lg[:, :, :], lg[:, :, :], rb2[:, 1, :].unsqueeze(1).to_broadcast(T), ALU.add))
                for r, sel in enumerate((s1, s2)):
                    c.link(V.tensor_reduce(rs[:, r, :], lg[:, :, :], AX, ALU.max))
                    c.link(V.tensor_tensor(rq[:, :, :], lg[:, :, :], rs[:, r, :].unsqueeze(2).to_broadcast(T),
                                           ALU.is_equal))
                    c.link(V.tensor_tensor(rq[:, :, :], rq[:, :, :], prio.unsqueeze(1).to_broadcast(T), ALU.mult))
                    c.link(V.tensor_reduce(rs[:, 4, :], rq[:, :, :], AX, ALU.max))
                    c.link(V.tensor_tensor(sel[:, :, :], rq[:, :, :], rs[:, 4, :].unsqueeze(2).to_broadcast(T),
                                           ALU.is_equal))
                    if r == 0:
                        c.link(V.scalar_tensor_tensor(out=lg[:, :, :], in0=s1[:, :, :], scalar=-1e30,
                                                      in1=lg[:, :, :], op0=ALU.mult, op1=ALU.add))
                V.tensor_tensor(rs[:, 2, :], rs[:, 1, :], rs[:, 0, :], ALU.subtract).then_inc(r_gap, 1)
                dve.wait_ge(r_exp, k + 1)
                c.link(V.tensor_scalar(rs[:, 5, :], rs[:, 3, :], 1.0, None, ALU.add))
                c.link(V.reciprocal(rs[:, 6, :], rs[:, 5, :]))
                c.link(V.tensor_tensor(rs[:, 7, :], rs[:, 6, :], rs[:, 3, :], ALU.mult))
                c.link(V.tensor_tensor(s1[:, :, :], s1[:, :, :], rs[:, 6, :].unsqueeze(2).to_broadcast(T), ALU.mult))
                c.link(V.tensor_tensor(s2[:, :, :], s2[:, :, :], rs[:, 7, :].unsqueeze(2).to_broadcast(T), ALU.mult))
                V.tensor_tensor(s1[:, :, :], s1[:, :, :], s2[:, :, :], ALU.add).then_inc(r_mask, 1)
                fsem, per = (dve_ffn, dve_bil)[k], 2 * NE + (nE - NE)
                credits, hold = dn, (3, 4)[k]
                dve.sem_inc(y_used[k], credits)
                with dve.Fori(0, NC // 2) as i:
                    for half in range(2):
                        q = 2 * i + half
                        f = Chain(dve, fsem, q * per)
                        dve.wait_ge(mB_in[k][half], (i + 1) * (16 * NE))
                        for e in range(nE):
                            xq = xT[:, nlast(q)]
                            dve.wait_ge(down_done[k], q * nE + hold + e + 1)
                            y = psum[:, 4 + e % dn, :]
                            if e < nE - NE:
                                f.link(V.scalar_tensor_tensor(out=xq, in0=y, scalar=fB2[:, e:e + 1], in1=xq,
                                                              op0=ALU.add, op1=ALU.add))
                            else:
                                f.link(V.scalar_tensor_tensor(out=yT[e % 2][:, :], in0=y, scalar=fB2[:, e:e + 1],
                                                              in1=mB[:, half * NE + e - (nE - NE), :], op0=ALU.add,
                                                              op1=ALU.mult))
                                f.link(V.tensor_tensor(xq, xq, yT[e % 2][:, :], ALU.add))
                            dve.sem_inc(y_used[k], 1)
                        assert f.n == per

            ln_vector(1)
            ffn_vector(0, FFN0[0])
            ln_vector(2)
            dve.wait_ge(b_hi, 3)
            c.link(V.tensor_tensor(h3b[1][:, :], hT[:, :], h3b[0][:, :], ALU.subtract))
            c.link(V.tensor_tensor(bw2[1][:, :], bw2f[:, :], bw2[0][:, :], ALU.subtract))
            V.tensor_tensor(bw1b[1][:, :], bw1[:, :], bw1b[0][:, :], ALU.subtract).then_inc(b_split, 1)
            dve.sem_inc(b_prod, 1)
            with dve.Fori(0, NT // 2) as i:
                for s in range(2):
                    n = 2 * i + s
                    dve.wait_ge(b_node, n + 1)
                    V.tensor_copy(nodek[s][:, :], psum[:, 4 * s, 0:K1]).then_inc(b_x, 1)
                    dve.wait_ge(b_x, n * 3 + 1)
                    dve.wait_ge(b_ps, n + 1)
                    V.tensor_tensor(prod[s][:, :, :],
                                    psum[:, 4 * s:4 * s + 4, :].rearrange("p b (k f) -> p (b k) f", f=P),
                                    nodek[s][:, :].unsqueeze(2).to_broadcast([P, K1, P]), ALU.mult).then_inc(b_prod, 1)
                    dve.wait_ge(b_prod, n + 2)
                    c2 = V.tensor_reduce(xf[s][:, :], prod[s][:, :, :].rearrange("p k f -> p f k"), AX, ALU.add)
                    c2.then_inc(bf_consts, 1)
                    dve.wait_ge(bf_consts, n + 1)
                    V.tensor_copy(Xb[0][:, ds(n, 1), :].rearrange("p o f -> p (o f)"), xf[s][:, :]).then_inc(b_x, 1)
                    dve.wait_ge(b_x, n * 3 + 2)
                    V.tensor_tensor(Xb[1][:, ds(n, 1), :].rearrange("p o f -> p (o f)"), xf[s][:, :],
                                    Xb[0][:, ds(n, 1), :].rearrange("p o f -> p (o f)"), ALU.subtract).then_inc(b_x, 1)
            dve.wait_ge(wb_ps, 1)
            V.tensor_copy(wb[:, :], psum[:, 0, 0:P]).then_inc(wb_ok, 1)
            with dve.Fori(0, NT // 2) as i:
                for s in range(2):
                    dve.wait_ge(l_hi, 2 * i + s + 1)
                    dve.wait_ge(l_mm, 2 * i + s)
                    V.tensor_tensor(A4lo[s][:, :], A4[s][:, :], A4hi[s][:, :], ALU.subtract).then_inc(l_lo, 1)
            dve.wait_ge(l_mm, NT + 1)
            for q in range(NC):
                xq = xT[:, q * CH:(q + 1) * CH]
                V.scalar_tensor_tensor(out=xq, in0=psum[:, q, :], scalar=0.0, in1=xq, op0=ALU.max,
                                       op1=ALU.add).then_inc(l_add, 1)
            dve.wait_ge(l_add, NC)
            ln_vector(3)
            ffn_vector(1, FFN1[0])
            dve.wait_ge(dve_bil, NC * 2 * NE)
            dve.sem_inc(final, 1)


def kernel(**inputs):
    import numpy as np
    import concourse.bacc as bacc
    from concourse import mybir as mb
    from concourse.bass_utils import run_bass_kernel_spmd as run

    g = {k: np.asarray(v) for k, v in inputs.items()}

    def tiles_last(b, n):
        return b.reshape(n, P).T

    def expert_w1(w):
        return w.transpose(1, 0, 2).reshape(P, -1)

    def expert_w2(w):
        e, f, d = w.shape
        return w.reshape(e, f // P, P, d).transpose(2, 0, 1, 3).reshape(P, -1)

    consts = np.zeros((P, C_END), np.float32)
    consts[:, C_ID:C_ID + P] = np.eye(P)
    consts[:, C_OFF:C_OFF + P] = 1 - np.eye(P)
    consts[:, C_ONE:C_ONE + P] = 1
    for h in range(HEADS):
        for part in range(2):
            rows = slice(part * PART + h * KL, part * PART + (h + 1) * KL)
            consts[rows, C_SD + 3 + h] = 1
            if part == 0:
                consts[rows, C_SC + h] = 1
    consts[:, C_KK:C_KK + KL] = np.arange(KL)
    consts[:, C_PR:C_PR + NE] = NE - np.arange(NE)
    consts[:, C_SG], consts[:, C_SG + 1] = 1, -1

    p0, p1, q0, q1 = "L0_gnn_", "L0_ffn_", "L1_gnn_", "L1_ffn_"
    arrays = {
        "consts": consts,
        "xT": g["x"].T,
        "adjT": g["adj"].T,
        "gatW": g[p0 + "gat_W"].transpose(1, 0, 2).reshape(P, -1),
        "gatWT": g[p0 + "gat_W"].transpose(2, 0, 1).reshape(P, -1),
        "gatA": g[p0 + "gat_a"].reshape(HEADS, 2, P).transpose(2, 0, 1),
        "gruW": np.stack([g[p0 + n].T for n in ("edge_Wih", "edge_Whh", "node_Wih", "node_Whh")], 1),
        "gruB": np.stack([tiles_last(g[p0 + n], 3) for n in ("edge_bih", "edge_bhh", "node_bih", "node_bhh")], 1),
        "Wr_0": g[p1 + "Wr"],
        "rb_0": np.zeros((2, NE), np.float32),
        "W1_0": np.concatenate([g[p1 + "W1s"], expert_w1(g[p1 + "W1p"])], 1),
        "W2_0": np.concatenate([expert_w2(g[p1 + "W2s"][None]), expert_w2(g[p1 + "W2p"])], 1),
        "B1_0": np.concatenate([tiles_last(g[p1 + "b1s"], 4), tiles_last(g[p1 + "b1p"].reshape(-1), 32)], 1),
        "B2_0": np.concatenate([g[p1 + "b2s"][:, None], g[p1 + "b2p"].T], 1),
        "b_W1": g[q0 + "W1"],
        "b_W1T": g[q0 + "W1"].T,
        "b_W2": g[q0 + "W2"].transpose(1, 0, 2).reshape(P, -1),
        "b_b": g[q0 + "b"],
        "Wr_1": g[q1 + "Wg"],
        "rb_1": np.stack([g[q1 + "bg"], g[q1 + "bias"]]),
        "W1_1": expert_w1(g[q1 + "W1"]),
        "W2_1": expert_w2(g[q1 + "W2"]),
        "B1_1": tiles_last(g[q1 + "b1"].reshape(-1), 16),
        "B2_1": g[q1 + "b2"].T,
    }
    nc = bacc.Bacc("TRN2", target_bir_lowering=False, num_devices=1)
    sent, aps = {}, {}
    for name, v in arrays.items():
        v = np.ascontiguousarray(v)
        sent["in_" + name] = v
        aps[name] = nc.dram_tensor("in_" + name, v.shape, mb.dt.from_np(v.dtype), kind="ExternalInput").ap()
    out = nc.dram_tensor("out_xT", (P, N), F32, kind="ExternalOutput").ap()
    build(nc, aps, out)
    r = run(nc, [sent], core_ids=[0])
    return np.ascontiguousarray(r.results[0]["out_xT"].T)
```

```python
import math
from contextlib import ExitStack

import concourse.bass as bass
from concourse import mybir

F32, BF16, FP16 = mybir.dt.float32, mybir.dt.bfloat16, mybir.dt.float16
I32, I16, U8 = mybir.dt.int32, mybir.dt.int16, mybir.dt.uint8
BYTES = {F32: 4, BF16: 2, FP16: 2, I32: 4, I16: 2, U8: 1}
ALU = mybir.AluOpType
ACT = mybir.ActivationFunctionType
AX = mybir.AxisListType.X
ROP = bass.bass_isa.ReduceOp
ds = bass.ds

P = 128
N = 4096
NT = N // P
CH = 512
NC = N // CH
HEADS = 3
RB = 1024
NRB = N // RB
HB = 4
TS = 4
TPB = RB // P
LEVEL = 64
KL = 21
PART = KL * HEADS
POISON = float(2.0 ** 60)
CLEAN = float(2.0 ** 40)
LN2 = math.log(2.0)
LN2_HI = 355.0 / 512.0
LN2_LO = LN2 - LN2_HI
ROUND = float(1.5 * 2 ** 23)
TINY = 1e-30
EPS = 1e-5
SLOPE = 0.2
K1 = 16
NE = 8
FFN0 = (9, 4)
FFN1 = (8, 2)

C_ID, C_OFF, C_ONE, C_SD, C_SC, C_KK, C_PR, C_SG, C_AV, C_END = (
    0, 128, 256, 384, 390, 396, 417, 425, 427, 555)

SCRATCH = "Internal"
STOP = 99


def build(nc, a, out):
    with ExitStack() as ctx:
        base = (nc.sbuf_base + 63) // 64 * 64
        KB = 1024
        small = [base]
        R = base + 6 * KB

        def sb(name, shape, dt, kb=None):
            size = BYTES[dt] * math.prod(shape[1:])
            if kb is None:
                off = small[0]
                small[0] = (off + size + 63) // 64 * 64
                assert small[0] <= R
            else:
                off = R + int(kb * KB)
            return nc.alloc_sbuf_tensor_at(name, shape, dt, offset=off)

        def sem(name):
            return ctx.enter_context(nc.semaphore(name))

        def dram(name, shape, dt):
            return nc.dram_tensor(name, shape, dt, kind=SCRATCH).ap()

        class Chain:

            def __init__(self, eng, s, start=0):
                self.eng, self.s, self.start, self.n = eng, s, start, 0

            def link(self, ins):
                ins.then_inc(self.s, 1)
                self.n += 1
                self.eng.wait_ge(self.s, self.start + self.n)

        cst = sb("cst", [P, C_END], F32)
        ident, offd = cst[:, C_ID:C_ID + P], cst[:, C_OFF:C_OFF + P]
        ones = cst[:, C_ONE:C_ONE + P]
        selD, selCf = cst[:, C_SD:C_SD + 6], cst[:, C_SC:C_SC + 6]
        kk, prio = cst[:, C_KK:C_KK + KL], cst[:, C_PR:C_PR + NE]
        sgn = cst[:, C_SG:C_SG + 2]
        mean = cst[:, C_AV:C_AV + P]
        selC = sb("selC", [P, 6], BF16)
        dpt = sb("dpt", [P, 2 * NT * HEADS], F32)
        wm = sb("wm", [P, 2 * NT * HEADS], F32)
        lev = sb("lev", [P, KL], F32)
        nsg = sb("nsg", [P, 3], I32)
        sm = sb("sm", [P, 16], F32)
        stat = sb("stat", [P, 6, NT], F32)
        zero = sb("zero", [P, CH], BF16)

        xT = sb("xT", [P, N], F32, 0)
        hT = sb("hT", [P, N], F32, 16)
        hn = sb("hn", [P, NT, P], F32, 32)
        sq = sb("sq", [P, NT // 2, P], F32, 48)
        hc = sb("hc", [P, N], F32, 32)
        sqT = [sb(f"sqT{i}", [P, CH], F32, 48 + 2 * i) for i in range(4)]
        gwTt = sb("gwTt", [P, HEADS * P], F32, 56)
        ga = sb("ga", [P, HEADS, 2], F32, 58)
        wa = sb("wa", [P, 2, HEADS], F32, 58.25)
        uvr = sb("uvr", [P, NT, 6], F32, 59)
        keep = sb("keep", [P, NT * N], U8, 0)
        Pb = [sb(f"Pb{i}", [P, N], BF16, 128 + 8 * i) for i in range(2)]
        Ar = [sb(f"Ar{i}", [P, N], F32, 144 + 16 * i) for i in range(2)]
        Pb += [sb(f"Pb{i}", [P, N], BF16, 144 + 8 * (i - 2)) for i in (2, 3)]
        junk = sb("junk", [P, N], BF16, 176)
        uvs = sb("uvs", [P, NT, 3, 6], BF16, 184)
        uvx = sb("uvx", [P, NT, 3, 6], BF16, 186)
        negs = sb("negs", [P, NT], F32, 188)
        zs = sb("zs", [P, NT, 18], F32, 144)
        z6 = sb("z6", [P, NT, 6], F32, 147)
        e6 = sb("e6", [P, 2, NT * HEADS], F32, 148)
        q6 = sb("q6", [P, 2, NT * HEADS], F32, 149)
        f6 = sb("f6", [P, 2, NT * HEADS], F32, 150)
        lvU = sb("lvU", [P, NT * HEADS, KL], F32, 144)
        lvE = sb("lvE", [P, NT * HEADS, KL], F32, 152)
        lvW = sb("lvW", [P, NT * HEADS, KL], F32, 160)
        lvP = sb("lvP", [P, NT * HEADS, KL], F32, 168)
        lw = sb("lw", [P, NT, P], BF16, 176)
        lsum = sb("lsum", [P, N], F32, 144)
        lind = sb("lind", [P, N], BF16, 160)
        acc6 = sb("acc6", [6, N], F32, 184)
        kr16 = sb("kr16", [6, N], I16, 144)
        den96 = sb("den96", [96, P], F32, 152)
        hn2 = sb("hn2", [P, NT * P], F32, 48)
        gw = sb("gw", [P, HEADS * P], F32, 168)
        gwb = [sb(f"gwb{i}", [P, HEADS * P], BF16, 169.5 + .75 * i) for i in range(2)]
        hTs = [sb(f"hTs{i}", [P, N], BF16, 32 + 8 * i) for i in range(2)]
        tf = [sb(f"tf{i}", [P, HEADS + 1, P], F32, 124 + 2 * i) for i in range(TS)]
        tb = [sb(f"tb{i}", [P, HEADS + 1, 2, P], BF16, 172 + 2 * i) for i in range(TS)]
        Ab = [sb(f"Ab{i}", [P, RB], F32, 32 + 4 * i) for i in range(2)]
        Ahi = [sb(f"Ahi{i}", [P, RB], BF16, 40 + 2 * i) for i in range(2)]
        Alo = [sb(f"Alo{i}", [P, RB], BF16, 44 + 2 * i) for i in range(2)]
        Tt = [sb(f"Tt{i}", [P, HEADS + 1, 2, P], BF16, 48 + 2 * i) for i in range(2)]
        tt = [sb(f"tt{i}", [P, HEADS, RB], FP16, 52 + 6 * i) for i in range(2)]
        ss = [sb(f"ss{i}", [P, HEADS, RB], BF16, 64 + 6 * i) for i in range(2)]
        ph = [sb(f"ph{i}", [P, HEADS, RB], BF16, 76 + 6 * i) for i in range(2)]
        pl = [sb(f"pl{i}", [P, HEADS, RB], BF16, 88 + 6 * i) for i in range(2)]
        KR = sb("KR", [P, HEADS, N], I16, 100)
        RD = sb("RD", [P, HEADS, RB], F32, 124)
        esP = sb("esP", [P, HEADS, N], F32, 136)
        esT = esP[:, 0, :]
        nsT = sb("nsT", [P, N], F32, 184)
        dB = sb("dB", [P, N], F32, 104)
        gruW = sb("gruW", [P, 4, 3 * P], F32, 32)
        gruB = sb("gruB", [P, 4, 3], F32, 39)
        gbr = sb("gbr", [P, 2, 2], F32, 39.5)
        gR = [sb(f"gR{i}", [P, CH], F32, 40 + 2 * i) for i in range(2)]
        gZ = [sb(f"gZ{i}", [P, CH], F32, 44 + 2 * i) for i in range(2)]
        gM = [sb(f"gM{i}", [P, CH], F32, 48 + 2 * i) for i in range(2)]
        gU = [sb(f"gU{i}", [P, CH], F32, 52 + 2 * i) for i in range(2)]
        Wr = sb("Wr", [P, NE], F32, 56)
        rb2 = sb("rb2", [P, 2, NE], F32, 56.25)
        lg = sb("lg", [P, NT, NE], F32, 57)
        rq = sb("rq", [P, NT, NE], F32, 58)
        s1 = sb("s1", [P, NT, NE], F32, 59)
        s2 = sb("s2", [P, NT, NE], F32, 60)
        rs = sb("rs", [P, 8, NT], F32, 61)
        mk8 = sb("mk8", [NE, N], F32, 32)
        fWs = [sb(f"fWs{i}", [P, 18 * KB // 4], F32, 64 + 18 * i) for i in range(2)]
        fB1 = sb("fB1", [P, 36], F32, 100)
        fB2 = sb("fB2", [P, 9], F32, 100.5)
        hTp = [sb(f"hTp{i}", [P, N], BF16, 101 + 8 * i) for i in range(2)]
        hid = [sb(f"hid{i}", [P, CH], F32, 117 + 2 * i) for i in range(HB)]
        mB = sb("mB", [P, 2 * NE, CH], F32, 126)
        yT = [sb(f"yT{i}", [P, CH], F32, 158 + 2 * i) for i in range(2)]
        fW = [[sb(f"fW{i}{j}", [P, 18 * KB // 4], BF16, 162 + 18 * i + 9 * j) for j in range(2)]
              for i in range(2)]
        hidp = [sb(f"hidp{i}", [P, 2, CH], BF16, 64 + 2 * i) for i in range(12)]
        bw2f = sb("bw2f", [P, K1 * P], F32, 64)
        bw2 = [sb(f"bw2{i}", [P, K1 * P], BF16, 72 + 4 * i) for i in range(2)]
        bw1 = sb("bw1", [P, K1], F32, 80)
        bw1b = [sb(f"bw1b{i}", [P, K1], BF16, 80.25 + .25 * i) for i in range(2)]
        bw1T = sb("bw1T", [K1, P], F32, 81)
        bb = sb("bb", [K1, P], F32, 81.5)
        wb = sb("wb", [P, P], F32, 82)
        h3b = [sb(f"h3b{i}", [P, N], BF16, 84 + 8 * i) for i in range(2)]
        prod = [sb(f"prod{i}", [P, K1, P], F32, 100 + 8 * i) for i in range(2)]
        nodek = sb("nodek", [P, NT, K1], F32, 116)
        xf = [sb(f"xf{i}", [P, P], F32, 118 + .5 * i) for i in range(2)]
        halves = [sb(f"halves{i}", [P, K1 // 2, P], F32, 119 + 4 * i) for i in range(2)]
        Xb = [sb(f"Xb{i}", [P, NT, P], BF16, 48 + 8 * i) for i in range(2)]
        A4 = [sb(f"A4{i}", [P, N], F32, kb) for i, kb in enumerate((128, 144, 32, 64))]
        A4hi = [sb(f"A4hi{i}", [P, N], BF16, kb) for i, kb in enumerate((160, 168, 84, 92))]
        A4lo = [sb(f"A4lo{i}", [P, N], BF16, kb) for i, kb in enumerate((176, 184, 100, 108))]

        psum = ctx.enter_context(nc.psum_tensor("psum", [P, NC, CH], F32))
        flat = psum[:, :, :].rearrange("p b c -> p (b c)")

        hT_d, hn_d = dram("hT_d", [P, N], F32), dram("hn_d", [P, N], F32)
        diag_d = dram("diag_d", [N], F32)
        kr_d = dram("kr_d", [HEADS, N], I16)
        den_d, rden_d = dram("den_d", [HEADS, N], F32), dram("rden_d", [HEADS, N], F32)
        T_d = dram("T_d", [2 * NT * P, (HEADS + 1) * 2 * P], BF16)
        mk_d = [dram(f"mk_d{i}", [NE, N], F32) for i in range(2)]
        adj, adj_f = a["adjT"], a["adjT"].rearrange("a b -> (a b)")

        def S(*names):
            return [sem(n) for n in names]

        cst_in, x_in, gat_in, spilled = S("cst_in", "x_in", "gat_in", "spilled")
        dve_steps, dve_lv, dve_ffn0, dve_gru, dve_ffn1 = S("dve_steps", "dve_lv", "dve_ffn0", "dve_gru", "dve_ffn1")
        ln_turned, ln_centred, ln_squared, ln_var, ln_std, ln_normed, ln_back, ln_done = S(
            "ln_turned", "ln_centred", "ln_squared", "ln_var", "ln_std", "ln_normed", "ln_back", "ln_done")
        lt_mean, lt_centred, lt_squared, lt_sum = S("lt_mean", "lt_centred", "lt_squared", "lt_sum")
        uv_ps, uv_ok = S("uv_ps", "uv_ok")
        m_in = S("m_in0", "m_in1")
        m_diag, m_mask, m_kept, m_neg, m_sum = S("m_diag", "m_mask", "m_kept", "m_neg", "m_sum")
        neg_rows, neg_tot, nsign_ok, x_sum, x_in2, x_mask, x_diag = S(
            "neg_rows", "neg_tot", "nsign_ok", "x_sum", "x_in2", "x_mask", "x_diag")
        range_l, range_g, groups_ok, frac_ok, wm_ok = S(
            "range_l", "range_g", "groups_ok", "frac_ok", "wm_ok")
        lv_cap, lv_exp, lv_w, lv_conv0, lv_conv1, lv_sum, lv_copied, lv_ind, lv_sel = S(
            "lv_cap", "lv_exp", "lv_w", "lv_conv0", "lv_conv1", "lv_sum", "lv_copied", "lv_ind", "lv_sel")
        ly_in, ly_mask, ly_sum, ly_diag, ly_w, ly_cap, ly_exp, lv_all, dve_ly = S(
            "ly_in", "ly_mask", "ly_sum", "ly_diag", "ly_w", "ly_cap", "ly_exp", "lv_all", "dve_ly")
        kr_ok, kr_out, den_out, den_back, rden_ok, rden_out, att_in = S(
            "kr_ok", "kr_out", "den_out", "den_back", "rden_ok", "rden_out", "att_in")
        th_in, th_hi, th_lo = S("th_in", "th_hi", "th_lo")
        t_ps, t_mul, t_slot3, t_hi, t_lo = S("t_ps", "t_mul", "t_slot3", "t_hi", "t_lo")
        t_out = S(*[f"t_out{s}" for s in range(TS)])
        a_in, at_in = S("a_in0", "a_in1"), S("at_in0", "at_in1")
        a_prep, a_relu, a_hi, a_lo, a_t, a_s, a_ph, a_pl, a_mm = S(
            "a_prep", "a_relu", "a_hi", "a_lo", "a_t", "a_s", "a_ph", "a_pl", "a_mm")
        rd_in, ns_out, es_out, es_add, es_ok = S("rd_in", "ns_out", "es_out", "es_add", "es_ok")
        gbr_ok, g_in, g_ps, g_gate, g_nin, g_tanh, g_new, g_scaled, g_used, dve_upd, seen = S(
            "gbr_ok", "g_in", "g_ps", "g_gate", "g_nin", "g_tanh", "g_new", "g_scaled", "g_used", "dve_upd", "seen")
        r_in, r_ps, r_gap, r_exp, r_mask, r_tr, r_mk8, r_out = S(
            "r_in", "r_ps", "r_gap", "r_exp", "r_mask", "r_tr", "r_mk8", "r_out")
        up_done, act_done, down_done, y_used = [S(f"{n}_0", f"{n}_1") for n in
                                                ("up_done", "act_done", "down_done", "y_used")]
        hid_hi, hid_lo = [S(f"{n}_0", f"{n}_1") for n in ("hid_hi", "hid_lo")]
        fw_hi, fh_hi, f_lo = S("fw_hi", "fh_hi", "f_lo")
        mB_in = [S("mB_in00", "mB_in01"), S("mB_in10", "mB_in11")]
        b_in, b_hi, b_split, b_w_lo, b_ps, b_node, b_node_ok, b_prod_a, b_prod_d, b_half, b_sum, b_x_hi, b_x = S(
            "b_in", "b_hi", "b_split", "b_w_lo", "b_ps", "b_node", "b_node_ok", "b_prod_a", "b_prod_d", "b_half", "b_sum",
            "b_x_hi", "b_x")
        l_in = S("l_in0", "l_in1", "l_in2", "l_in3")
        l_hi, l_lo, l_mm, l_add = S("l_hi", "l_lo", "l_mm", "l_add")
        out_done, = S("out_done")

        def nlast(q):
            return ds(q * CH, CH)

        block = ctx.enter_context(nc.Block())

        @block.sync
        def _(sp):
            sp.dma_start(cst[:, :], a["consts"]).then_inc(cst_in, 16)
            sp.dma_start(xT[:, :], a["xT"]).then_inc(x_in, 16)
            sp.dma_start(gwTt[:, :], a["gatWT"]).then_inc(gat_in, 16)
            sp.dma_start(ga[:, :, :], a["gatA"]).then_inc(gat_in, 16)
            with nc.allow_non_contiguous_dma(reason="the diagonal of adj"):
                sp.dma_start(diag_d.rearrange("(a b) -> a b", a=16),
                             bass.AP(adj.tensor, 0, [[256 * (N + 1), 16], [N + 1, 256]])).then_inc(spilled, 16)
            sp.wait_ge(ln_done, 2)
            sp.dma_start(hT_d, hT[:, :]).then_inc(spilled, 16)
            sp.dma_start(hn_d, hn[:, :, :].rearrange("p t f -> p (t f)")).then_inc(spilled, 16)

            for s in range(2):
                sp.dma_start(Ar[s][:, :], adj[s * P:(s + 1) * P, :]).then_inc(m_in[s], 16)
            with sp.Fori(1, NT // 2) as i:
                for s in range(2):
                    sp.wait_ge(m_mask, 2 * i + s)
                    sp.wait_ge(m_neg, 2 * i + s)
                    sp.dma_start(Ar[s][:, :], adj[ds((2 * i + s) * P, P), :]).then_inc(m_in[s], 16)
            sp.wait_ge(nsign_ok, 1)
            nsign = sp.value_load(nsg[0:1, 0:1], min_val=1, max_val=2)
            with sp.If(nsign == 2):
                with sp.Fori(0, NT) as t:
                    sp.wait_ge(x_mask, t + 1)
                    sp.dma_start(Ar[0][:, :], adj[ds(t * P, P), :]).then_inc(x_in2, 16)

            sp.wait_ge(groups_ok, 1)
            groups = sp.value_load(nsg[0:1, 1:2], min_val=1, max_val=1 << 20)
            with sp.If(nsign == 2):
                with sp.Fori(0, groups) as g:
                    with sp.Fori(0, NT) as t:
                        sp.wait_ge(ly_w, g + 1)
                        sp.wait_ge(ly_mask, g * NT + t + 1)
                        sp.dma_start(Ar[0][:, :], adj[ds(t * P, P), :]).then_inc(ly_in, 16)

            sp.wait_ge(lv_all, groups)
            sp.dma_start(hT[:, :], hT_d).then_inc(th_in, 16)
            sp.dma_start(gw[:, :], a["gatW"]).then_inc(th_in, 16)
            sp.dma_start(hn2[:, :], hn_d).then_inc(att_in, 16)
            sp.wait_ge(kr_ok, 1)
            sp.dma_start(den_d, acc6[3:6, :]).then_inc(den_out, 16)
            sp.dma_start(kr_d, kr16[0:3, :]).then_inc(kr_out, 16)
            sp.wait_ge(den_out, 16)
            sp.dma_start(den96[:, :], den_d.rearrange("i (a b) -> (i a) b", b=P)).then_inc(den_back, 16)
            sp.wait_ge(kr_out, 16)
            sp.dma_start(KR[:, :, :].rearrange("p i n -> p (i n)"),
                         kr_d.rearrange("i n -> (i n)").partition_broadcast(P)).then_inc(kr_out, 16)
            with sp.Fori(0, nsign) as sg:
                with sp.Fori(0, NT // TS) as i:
                    for s in range(TS):
                        sp.wait_ge(t_lo, sg * NT + TS * i + s + TS + 1)
                        sp.dma_start(T_d[ds((sg * NT + TS * i + s) * P, P), :],
                                     tb[s][:, :, :, :].rearrange("p h l f -> p (h l f)")).then_inc(t_out[s], 16)
            for s in range(TS):
                sp.wait_ge(t_out[s], nsign * (16 * NT // TS) + 16)
                sp.sem_inc(seen, 1)
            sp.wait_ge(rden_ok, 1)
            sp.dma_start(rden_d.rearrange("i (a b) -> (i a) b", b=P), den96[:, :]).then_inc(rden_out, 16)
            sp.dma_start(xT[:, :], a["xT"]).then_inc(x_in, 16)
            sp.wait_ge(rden_out, 16)

            with sp.Fori(0, NRB) as rb:
                with sp.Fori(0, nsign) as sg:
                    with sp.Fori(0, NT // 2) as i:
                        for s in range(2):
                            n = (rb * nsign + sg) * NT + 2 * i + s
                            sp.wait_ge(a_lo, n + 1)
                            sp.dma_start(Ab[s][:, :], adj[ds((2 * i + s) * P, P), ds(rb * RB, RB)]
                                         ).then_inc(a_in[s], 16)
                            sp.wait_ge(a_mm, n + 1)
                            sp.dma_start(Tt[s][:, :, :, :].rearrange("p h l f -> p (h l f)"),
                                         T_d[ds((sg * NT + 2 * i + s) * P, P), :]).then_inc(at_in[s], 16)
                sp.wait_ge(es_out, rb + 1)
                for h in range(HEADS):
                    sp.dma_start(RD[:, h, :], rden_d[h:h + 1, ds(rb * RB, RB)]
                                 .rearrange("o n -> (o n)").partition_broadcast(P)).then_inc(rd_in, 16)

            sp.wait_ge(es_out, NRB + 1)
            sp.dma_start(gruW[:, :, :], a["gruW"]).then_inc(g_in, 16)
            sp.dma_start(gruB[:, :, :], a["gruB"]).then_inc(g_in, 16)
            sp.dma_start(dB[:, :], diag_d.partition_broadcast(P)).then_inc(g_in, 16)

            def ffn_loads(k, nE, nF):
                if k == 1:
                    sp.wait_ge(l_mm, NT + 4)
                for name, tile in (("Wr", Wr[:, :]), ("rb", rb2[:, :, :]),
                                   ("W1", fWs[0][:, 0:nE * nF * P]), ("W2", fWs[1][:, 0:nE * nF * P]),
                                   ("B1", fB1[:, 0:nE * nF]), ("B2", fB2[:, 0:nE])):
                    src = a[f"{name}_{k}"]
                    if name == "rb":
                        src = src.rearrange("a e -> (a e)").partition_broadcast(P)
                        tile = rb2[:, :, :].rearrange("p a e -> p (a e)")
                    sp.dma_start(tile, src).then_inc(r_in, 16)
                sp.wait_ge(r_mk8, 4 * k + 4)
                sp.dma_start(mk_d[k], mk8[:, :]).then_inc(r_out, 16)
                sp.wait_ge(r_out, 16 * (k + 1))
                first = nE - NE
                def weights(s, q):
                    for e in range(NE):
                        sp.dma_start(mB[:, NE * s + e, :], mk_d[k][e, ds(q * CH, CH)].partition_broadcast(P)
                                     ).then_inc(mB_in[k][s], 16)

                weights(0, 0)
                weights(1, 1)
                with sp.Fori(1, NC // 2) as i:
                    for s in range(2):
                        sp.wait_ge(y_used[k], (2 * i + s - 1) * nE + (3, 4)[k])
                        weights(s, 2 * i + s)

            ffn_loads(0, *FFN0)
            sp.wait_ge(dve_ffn0, NC * (2 * NE + 1))
            sp.dma_start(bw2f[:, :], a["b_W2"]).then_inc(b_in, 16)
            sp.dma_start(bw1[:, :], a["b_W1"]).then_inc(b_in, 16)
            sp.dma_start(bw1T[:, :], a["b_W1T"]).then_inc(b_in, 16)
            sp.dma_start(bb[:, :], a["b_b"]).then_inc(b_in, 16)
            sp.wait_ge(ln_done, 2 + 2 * NC)
            for s in range(4):
                if s == 3:
                    sp.wait_ge(b_x, NT + 2)
                sp.dma_start(A4[s][:, :], adj[s * P:(s + 1) * P, :]).then_inc(l_in[s], 16)
            with sp.Fori(1, NT // 4) as i:
                for s in range(4):
                    sp.wait_ge(l_lo, 4 * i + s - 3)
                    sp.dma_start(A4[s][:, :], adj[ds((4 * i + s) * P, P), :]).then_inc(l_in[s], 16)
            ffn_loads(1, *FFN1)
            sp.wait_ge(dve_ffn1, NC * 2 * NE)
            sp.dma_start(out, xT[:, :]).then_inc(out_done, 16)
            sp.wait_ge(out_done, 16)
            sp.wait_ge(spilled, 48)

        @block.gpsimd
        def _(pool):
            pool.wait_ge(range_l, 1)
            pool.partition_all_reduce(sm[:, 3:6], sm[:, 0:3], P, ROP.max).then_inc(range_g, 1)
            pool.wait_ge(range_l, 2)
            pool.partition_all_reduce(sm[:, 7:8], sm[:, 6:7], P, ROP.max).then_inc(range_g, 1)
            pool.wait_ge(th_hi, 1)
            pool.tensor_tensor(gwb[1][:, :], gw[:, :], gwb[0][:, :], ALU.subtract).then_inc(th_lo, 1)
            pool.wait_ge(th_hi, 2)
            pool.tensor_tensor(hTs[1][:, :], hT[:, :], hTs[0][:, :], ALU.subtract).then_inc(th_lo, 1)
            pool.wait_ge(nsign_ok, 1)
            nsign = pool.value_load(nsg[0:1, 0:1], min_val=1, max_val=2)
            pool.sem_inc(a_lo, 2)
            for rb in range(NRB):
                with pool.Fori(0, nsign) as sg:
                    for lo, hi in ((0, rb * TPB), (rb * TPB, rb * TPB + TPB), (rb * TPB + TPB, NT)):
                        if lo == hi:
                            continue
                        diagonal = lo == rb * TPB
                        with pool.Fori(lo // 2, hi // 2) as i:
                            for s in range(2):
                                n = (rb * nsign + sg) * NT + 2 * i + s
                                pool.wait_ge(a_in[s], ((rb * nsign + sg) * (NT // 2) + i) * 16 + 16)
                                if diagonal:
                                    blk = Ab[s][:, ds((2 * i + s - rb * TPB) * P, P)]
                                    pool.tensor_tensor(blk, blk, offd, ALU.mult).then_inc(a_prep, 1)
                                else:
                                    pool.sem_inc(a_prep, 1)
                                pool.wait_ge(a_hi, n + 1)
                                pool.wait_ge(a_mm, n + 1)
                                pool.tensor_tensor(Alo[s][:, :], Ab[s][:, :], Ahi[s][:, :], ALU.subtract
                                                   ).then_inc(a_lo, 1)

            pool.wait_ge(es_out, NRB + 1)
            for q in range(NC):
                c = slice(q * CH, (q + 1) * CH)
                pool.tensor_tensor(esT[:, c], esT[:, c], esP[:, 1, c], ALU.add).then_inc(es_add, 1)
                pool.wait_ge(es_add, q + 1)
                pool.tensor_tensor(esT[:, c], esT[:, c], esP[:, 2, c], ALU.add).then_inc(es_ok, 1)
            pool.wait_ge(g_in, 48)
            pool.wait_ge(x_in, 32)
            pool.sem_inc(g_used, 2)
            with pool.Fori(0, NC) as q:
                for s in range(2):
                    n = 2 * q + s
                    pool.wait_ge(g_new, n + 3)
                    pool.sem_inc(seen, 1)
                    pool.tensor_tensor(gU[s][:, :], gU[s][:, :], dB[:, nlast(q)], ALU.mult).then_inc(g_scaled, 1)
                    pool.wait_ge(g_scaled, n + 1)
                    pool.wait_ge(g_used, n + 2)
                    pool.sem_inc(seen, 1)
                    pool.tensor_tensor(xT[:, nlast(q)], xT[:, nlast(q)], gU[s][:, :], ALU.add).then_inc(g_used, 1)

            def bilinear_weights():
                pool.wait_ge(b_hi, 1)
                pool.tensor_tensor(bw2[1][:, :], bw2f[:, :], bw2[0][:, :], ALU.subtract).then_inc(b_w_lo, 1)
                pool.wait_ge(b_hi, 2)
                pool.tensor_tensor(bw1b[1][:, :], bw1[:, :], bw1b[0][:, :], ALU.subtract).then_inc(b_w_lo, 1)

            def ffn_pool(k, nE, nF):
                ring = (12, 8)[k]

                def low_weights():
                    for i in range(2):
                        pool.wait_ge(fw_hi, 2 * k + i + 1)
                        pool.tensor_tensor(fW[i][1][:, 0:nE * nF * P], fWs[i][:, 0:nE * nF * P],
                                           fW[i][0][:, 0:nE * nF * P], ALU.subtract).then_inc(f_lo, 1)

                if k == 0:
                    low_weights()
                pool.wait_ge(fh_hi, k + 1)
                pool.tensor_tensor(hTp[1][:, :], hT[:, :], hTp[0][:, :], ALU.subtract).then_inc(f_lo, 1)
                if k == 1:
                    low_weights()
                pool.sem_inc(hid_lo[k], HB)
                with pool.Fori(0, NC) as q:
                    for j in range(nE * nF):
                        pool.wait_ge(hid_hi[k], q * (nE * nF) + j + 1)
                        pool.tensor_tensor(hidp[j % ring][:, 1, :], hid[j % HB][:, :], hidp[j % ring][:, 0, :],
                                           ALU.subtract).then_inc(hid_lo[k], 1)

            ffn_pool(0, *FFN0)

            bilinear_weights()
            def halve(n, s):
                pool.wait_ge(b_prod_a, n + 3)
                pool.wait_ge(b_prod_d, n + 3)
                pool.wait_ge(b_sum, n + 1)
                pool.tensor_tensor(halves[s][:, :, :], prod[s][:, 0:K1 // 2, :], prod[s][:, K1 // 2:, :],
                                   ALU.add).then_inc(b_half, 1)

            def split_x(n, s):
                hi = Xb[0][:, ds(n, 1), :].rearrange("p o f -> p (o f)")
                pool.wait_ge(b_x_hi, n + 1)
                pool.tensor_tensor(Xb[1][:, ds(n, 1), :].rearrange("p o f -> p (o f)"), xf[s][:, :], hi,
                                   ALU.subtract).then_inc(b_x, 1)

            pool.sem_inc(b_half, 2)
            pool.sem_inc(b_x, 2)
            halve(0, 0)
            with pool.Fori(0, NT // 2 - 1) as i:
                for s in range(2):
                    halve(2 * i + s + 1, 1 - s)
                    split_x(2 * i + s, s)
            halve(NT - 1, 1)
            split_x(NT - 2, 0)
            split_x(NT - 1, 1)
            ffn_pool(1, *FFN1)

        def ln_scalar(act):
            for hf in range(2):
                act.wait_ge(ln_centred, hf + 1)
                if hf == 1:
                    act.wait_ge(ln_var, 1)
                nc.scalar.activation(sq[:, :, :], hn[:, 16 * hf:16 * hf + 16, :], ACT.Square).then_inc(ln_squared, 1)
                act.wait_ge(ln_var, hf + 1)
                nc.scalar.activation(stat[:, 3, 16 * hf:16 * hf + 16], stat[:, 2, 16 * hf:16 * hf + 16],
                                     ACT.Sqrt).then_inc(ln_std, 1)
            for hf in range(2):
                act.wait_ge(ln_back, hf + 1)
                nc.scalar.activation(hT[:, hf * N // 2:(hf + 1) * N // 2], flat[:, hf * N // 2:(hf + 1) * N // 2],
                                     ACT.Copy).then_inc(ln_done, 1)

        def lt_scalar(act, k):
            for q in range(NC):
                act.wait_ge(lt_centred, NC * k + q + 1)
                if q >= 4:
                    act.wait_ge(lt_sum, NC * k + q - 3)
                nc.scalar.activation(sqT[q % 4][:, :], hc[:, q * CH:(q + 1) * CH],
                                     ACT.Square).then_inc(lt_squared, 1)
            act.wait_ge(ln_var, 3 + k)
            nc.scalar.activation(stat[:, 3, :], stat[:, 2, :], ACT.Sqrt).then_inc(ln_std, 1)

        @block.scalar
        def _(act):
            ln_scalar(act)
            act.sem_inc(m_neg, 1)
            with act.Fori(0, NT // 2) as i:
                for s in range(2):
                    act.wait_ge(m_diag, 2 * i + s + 1)
                    act.wait_ge(m_neg, 2 * i + s + 1)
                    nc.scalar.activation(junk[:, :], Ar[s][:, :], ACT.Relu, scale=-1.0,
                                         accum_out=negs[:, ds(2 * i + s, 1)]).then_inc(m_neg, 1)
            act.wait_ge(nsign_ok, 1)
            nsign = act.value_load(nsg[0:1, 0:1], min_val=1, max_val=2)
            signed = act.value_load(nsg[0:1, 2:3], min_val=0, max_val=1)
            act.wait_ge(frac_ok, 1)
            nc.scalar.activation(wm[:, :], f6[:, :, :].rearrange("p s t -> p (s t)"), ACT.Exp).then_inc(wm_ok, 1)
            act.wait_ge(groups_ok, 1)
            groups = act.value_load(nsg[0:1, 1:2], min_val=1, max_val=1 << 20)
            with act.Fori(0, groups) as g:
                act.wait_ge(lv_cap, g + 1)
                nc.scalar.activation(lvE[:, :, :], lvE[:, :, :], ACT.Exp, scale=LEVEL * LN2).then_inc(lv_exp, 1)
                with act.Fori(0, NT // 4) as i:
                    for s in (1, 3):
                        act.wait_ge(lv_w, g + 1)
                        act.wait_ge(lv_sum, g * NT + 4 * i + s + 1)
                        nc.scalar.activation(Pb[s][:, :], keep[:, ds((4 * i + s) * N, N)],
                                             ACT.Copy).then_inc(lv_conv1, 1)
                with act.If(nsign == 2):
                    act.wait_ge(ly_cap, g + 1)
                    nc.scalar.activation(lvE[:, :, :], lvE[:, :, :], ACT.Exp, scale=LEVEL * LN2).then_inc(ly_exp, 1)
                act.wait_ge(lv_all, g + 1)
                nc.scalar.activation(lsum[:, 0:N // 2], flat[:, 0:N // 2], ACT.Copy).then_inc(lv_copied, 1)

            act.wait_ge(th_in, 32)
            nc.scalar.activation(gwb[0][:, :], gw[:, :], ACT.Copy).then_inc(th_hi, 1)
            nc.scalar.activation(hTs[0][:, :], hT[:, :], ACT.Copy).then_inc(th_hi, 1)
            act.wait_ge(att_in, 16)
            for s in range(TS):
                act.sem_inc(t_out[s], 16)
            with act.Fori(0, nsign) as sg:
                with act.Fori(0, NT // TS) as i:
                    for s in range(TS):
                        n = sg * NT + TS * i + s
                        act.wait_ge(t_lo, n + 1)
                        nc.scalar.activation(tf[s][:, HEADS, :], hn2[:, ds((TS * i + s) * P, P)], ACT.Copy,
                                             scale=sgn[:, ds(sg, 1)]).then_inc(t_slot3, 1)
                        act.wait_ge(t_slot3, n + 1)
                        act.wait_ge(t_mul, n + TS + 1)
                        act.wait_ge(t_out[s], (sg * (NT // TS) + i) * 16 + 16)
                        nc.scalar.activation(tb[s][:, :, 0, :], tf[s][:, :, :], ACT.Copy).then_inc(t_hi, 1)

            act.sem_inc(a_s, 2)
            act.sem_inc(a_relu, 1)
            act.sem_inc(ns_out, 1)
            with act.Fori(0, NRB) as rb:
                with act.Fori(0, nsign) as sg:
                    with act.Fori(0, NT // 2) as i:
                        for s in range(2):
                            n = (rb * nsign + sg) * NT + 2 * i + s
                            act.wait_ge(a_t, n + 1)
                            act.wait_ge(a_pl, n + 1)
                            nc.scalar.activation(ss[s][:, :, :], tt[s][:, :, :], ACT.Exp,
                                                 scale=LEVEL * LN2).then_inc(a_s, 1)
                            with act.If(nsign == 2):
                                act.wait_ge(a_prep, n + 1)
                                nc.scalar.activation(Ab[s][:, :], Ab[s][:, :], ACT.Relu,
                                                     scale=sgn[:, ds(sg, 1)]).then_inc(a_relu, 1)
                            act.wait_ge(a_relu, signed * (n + 1) + 1)
                            act.wait_ge(a_prep, n + 1)
                            act.wait_ge(a_mm, n + 1)
                            nc.scalar.activation(Ahi[s][:, :], Ab[s][:, :], ACT.Copy).then_inc(a_hi, 1)
                act.wait_ge(a_mm, (rb + 1) * nsign * NT + 2)
                nc.scalar.activation(nsT[:, ds(rb * RB, RB)], flat[:, HEADS * RB:], ACT.Copy).then_inc(ns_out, 1)

            act.wait_ge(gbr_ok, 2)

            def gates(n, s):
                act.wait_ge(g_ps, n + 1)
                act.wait_ge(g_new, n + 1)
                nc.scalar.activation(gR[s][:, :], psum[:, 4 * s, :], ACT.Sigmoid,
                                     bias=gbr[:, s, 0:1]).then_inc(g_gate, 1)
                nc.scalar.activation(gZ[s][:, :], psum[:, 4 * s + 1, :], ACT.Sigmoid,
                                     bias=gbr[:, s, 1:2]).then_inc(g_gate, 1)

            def candidate(n, s):
                act.wait_ge(g_nin, n + 3)
                nc.scalar.activation(gM[s][:, :], gM[s][:, :], ACT.Tanh, bias=gruB[:, 2 * s, 2:3]).then_inc(g_tanh, 1)

            gates(0, 0)
            with act.Fori(0, NC - 1) as q:
                for s in range(2):
                    gates(2 * q + s + 1, 1 - s)
                    candidate(2 * q + s, s)
            gates(2 * NC - 1, 1)
            candidate(2 * NC - 2, 0)
            candidate(2 * NC - 1, 1)

            def ffn_weights(k, nE, nF):
                act.wait_ge(r_in, 96 * (k + 1))
                for i in range(2):
                    nc.scalar.activation(fW[i][0][:, 0:nE * nF * P], fWs[i][:, 0:nE * nF * P],
                                         ACT.Copy).then_inc(fw_hi, 1)

            def ffn_scalar(k, nE, nF, func):
                act.wait_ge(ln_done, 2 + NC * (2 * k + 1))
                nc.scalar.activation(hTp[0][:, :], hT[:, :], ACT.Copy).then_inc(fh_hi, 1)
                if k == 1:
                    ffn_weights(1, nE, nF)
                act.wait_ge(r_gap, k + 1)
                nc.scalar.activation(rs[:, 3, :], rs[:, 2, :], ACT.Exp).then_inc(r_exp, 1)
                for b in range(4):
                    act.wait_ge(r_tr, 4 * k + b + 1)
                    nc.scalar.activation(mk8[:, b * N // 4:(b + 1) * N // 4], flat[0:NE, b * N // 4:(b + 1) * N // 4],
                                         ACT.Copy).then_inc(r_mk8, 1)
                act.sem_inc(act_done[k], HB)
                with act.Fori(0, NC) as q:
                    for j in range(nE * nF):
                        act.wait_ge(hid_lo[k], q * (nE * nF) + j + 1)
                        act.wait_ge(up_done[k], q * (nE * nF) + j + 1)
                        nc.scalar.activation(hid[j % HB][:, :], psum[:, j % HB, :], func,
                                             bias=fB1[:, j:j + 1]).then_inc(act_done[k], 1)

            act.wait_ge(g_used, 2 * NC + 2)
            lt_scalar(act, 0)
            ffn_weights(0, *FFN0)
            ffn_scalar(0, *FFN0, ACT.Gelu)
            lt_scalar(act, 1)
            act.wait_ge(b_in, 64)
            nc.scalar.activation(bw2[0][:, :], bw2f[:, :], ACT.Copy).then_inc(b_hi, 1)
            nc.scalar.activation(bw1b[0][:, :], bw1[:, :], ACT.Copy).then_inc(b_hi, 1)
            for q in range(NC):
                act.wait_ge(ln_done, 3 + NC + q)
                nc.scalar.activation(h3b[0][:, q * CH:(q + 1) * CH], hT[:, q * CH:(q + 1) * CH],
                                     ACT.Copy).then_inc(b_hi, 1)
            act.wait_ge(b_node_ok, 1)
            act.sem_inc(b_prod_a, 2)
            with act.Fori(0, NT // 2) as i:
                for s in range(2):
                    n = 2 * i + s
                    act.wait_ge(b_ps, n + 1)
                    act.wait_ge(b_half, n + 1)
                    for k in range(K1 // 2):
                        last = nc.scalar.activation(
                            prod[s][:, k, :], psum[:, 4 * s + k // 4, k % 4 * P:k % 4 * P + P], ACT.Copy,
                            scale=nodek[:, ds(n, 1), k:k + 1].rearrange("p o k -> p (o k)"))
                    last.then_inc(b_prod_a, 1)
            act.wait_ge(b_x, NT + 2)
            with act.Fori(0, NT // 4) as i:
                for s in range(4):
                    act.wait_ge(l_in[s], i * 16 + 16)
                    act.wait_ge(l_mm, 4 * i + s + 1)
                    nc.scalar.activation(A4hi[s][:, :], A4[s][:, :], ACT.Copy).then_inc(l_hi, 1)
            lt_scalar(act, 2)
            ffn_scalar(1, *FFN1, ACT.Relu)

        def ln_tensor(pe):
            for hf in range(2):
                for t in range(16 * hf, 16 * hf + 16):
                    last = nc.tensor.transpose(flat[:, t * P:(t + 1) * P], xT[:, t * P:(t + 1) * P], ident)
                last.then_inc(ln_turned, 1)
            for hf in range(2):
                pe.wait_ge(ln_normed, hf + 1)
                for t in range(16 * hf, 16 * hf + 16):
                    last = nc.tensor.transpose(flat[:, t * P:(t + 1) * P], hn[:, t, :], ident)
                last.then_inc(ln_back, 1)

        def lt_tensor(pe, k):
            for q in range(NC):
                nc.tensor.matmul(psum[:, q, :], mean, xT[:, q * CH:(q + 1) * CH], start=True,
                                 stop=True).then_inc(lt_mean, 1)
            for q in range(NC):
                pe.wait_ge(lt_squared, NC * k + q + 1)
                for t in range(4):
                    last = nc.tensor.matmul(psum[:, 0, 4 * q + t:4 * q + t + 1], sqT[q % 4][:, t * P:(t + 1) * P],
                                            mean[:, 0:1], start=(q == 0 and t == 0), stop=True,
                                            skip_group_check=True)
                last.then_inc(lt_sum, 1)
            pe.wait_ge(ln_normed, 3 + k)
            for t in range(NT):
                last = nc.tensor.transpose(flat[:, t * P:(t + 1) * P], stat[:, 4, t:t + 1].to_broadcast([P, P]),
                                           ident)
                if t % 4 == 3:
                    last.then_inc(ln_back, 1)

        @block.tensor
        def _(pe):
            pe.wait_ge(cst_in, 16)
            pe.wait_ge(x_in, 16)
            ln_tensor(pe)
            pe.wait_ge(gat_in, 32)
            pe.wait_ge(ln_done, 2)
            for h in range(HEADS):
                last = nc.tensor.matmul(psum[:, 0, 2 * h:2 * h + 2], gwTt[:, h * P:(h + 1) * P], ga[:, h, :],
                                        start=(h == 0), stop=True, skip_group_check=True)
            last.then_inc(uv_ps, 1)
            pe.wait_ge(uv_ok, 1)
            for t in range(NT):
                last = nc.tensor.matmul(psum[:, 1, 6 * t:6 * t + 6], hT[:, t * P:(t + 1) * P],
                                        wa[:, :, :].rearrange("p a h -> p (a h)"),
                                        start=(t == 0), stop=True, skip_group_check=True)
            last.then_inc(uv_ps, 1)
            pe.wait_ge(uv_ok, 2)
            for b in range(2):
                nc.tensor.matmul(psum[:, b, 0:288], zero[:, 0:P], zero[:, 0:288], start=True, stop=False,
                                 skip_group_check=True)

            def sums(mask, uv, done):
                for t in range(NT):
                    last = nc.tensor.matmul(psum[:, t // 16, 18 * (t % 16):18 * (t % 16) + 18],
                                            mask[:, t * P:(t + 1) * P], uv,
                                            start=False, stop=False, skip_group_check=True)
                last.then_inc(done, 1)

            pe.sem_inc(m_sum, 2)
            pe.sem_inc(x_sum, 1)
            pe.sem_inc(ly_sum, 1)
            pe.sem_inc(lv_sum, 4)
            with pe.Fori(0, NT // 2) as i:
                for s in range(2):
                    pe.wait_ge(m_mask, 2 * i + s + 2)
                    sums(Pb[s], uvs[:, ds(2 * i + s, 1), :, :].rearrange("p o a b -> p (o a b)"), m_sum)
            pe.wait_ge(neg_rows, 1)
            nc.tensor.matmul(psum[:, 2, 0:1], ones, sm[:, 9:10], start=True, stop=True).then_inc(neg_tot, 1)
            pe.wait_ge(nsign_ok, 1)
            nsign = pe.value_load(nsg[0:1, 0:1], min_val=1, max_val=2)
            with pe.If(nsign == 2):
                with pe.Fori(0, NT) as t:
                    pe.wait_ge(x_mask, t + 2)
                    sums(Pb[0], uvx[:, ds(t, 1), :, :].rearrange("p o a b -> p (o a b)"), x_sum)

            pe.wait_ge(groups_ok, 1)
            groups = pe.value_load(nsg[0:1, 1:2], min_val=1, max_val=1 << 20)

            def levels(mask, t, done):
                for q in range(NC):
                    last = nc.tensor.matmul(psum[:, q, :], lw[:, ds(t, 1), :].rearrange("p o c -> p (o c)"),
                                            mask[:, q * CH:(q + 1) * CH], start=False, stop=False,
                                            skip_group_check=True)
                last.then_inc(done, 1)

            with pe.Fori(0, groups) as g:
                pe.wait_ge(lv_w, g + 1)
                pe.wait_ge(lv_ind, 3 * g + 1)
                for q in range(NC):
                    nc.tensor.matmul(psum[:, q, :], zero[:, 0:P], zero[:, :], start=True, stop=False,
                                     skip_group_check=True)
                with pe.Fori(0, NT // 4) as i:
                    for s in range(4):
                        pe.wait_ge((lv_conv0, lv_conv1)[s % 2], g * (NT // 2) + 2 * i + s // 2 + 1)
                        levels(Pb[s], 4 * i + s, lv_sum)
                with pe.If(nsign == 2):
                    with pe.Fori(0, NT) as t:
                        pe.wait_ge(ly_mask, g * NT + t + 2)
                        levels(Pb[0], t, ly_sum)
                nc.tensor.matmul(psum[:, 0, 0:1], zero[:, 0:P], zero[:, 0:1], start=False, stop=False,
                                 skip_group_check=True).then_inc(lv_all, 1)
                pe.wait_ge(lv_ind, 3 * g + 3)
                pe.wait_ge(lv_copied, g + 1)
                for q in range(NC):
                    nc.tensor.matmul(psum[0:6, q, :], selC[:, :], lind[:, q * CH:(q + 1) * CH], start=True,
                                     stop=False)
                    last = nc.tensor.matmul(psum[0:6, q, :], selD, lsum[:, q * CH:(q + 1) * CH], start=False,
                                            stop=True)
                last.then_inc(lv_sel, 1)

            pe.wait_ge(kr_ok, 1)
            pe.wait_ge(th_lo, 2)
            with pe.Fori(0, nsign) as sg:
                with pe.Fori(0, NT // TS) as i:
                    for s in range(TS):
                        n = sg * NT + TS * i + s
                        pe.wait_ge(t_mul, n + 1)
                        for w, (x, y) in enumerate(((0, 0), (0, 1), (1, 0))):
                            last = nc.tensor.matmul(psum[:, s, 0:HEADS * P], hTs[x][:, ds((TS * i + s) * P, P)],
                                                    gwb[y][:, :], start=(w == 0), stop=(w == 2))
                        last.then_inc(t_ps, 1)

            pe.sem_inc(a_mm, 2)
            with pe.Fori(0, NRB) as rb:
                pe.wait_ge(ns_out, rb + 1)
                pe.wait_ge(es_out, rb + 1)
                pe.wait_ge(t_lo, nsign * NT + TS)
                for q in range(NC):
                    nc.tensor.matmul(psum[:, q, :], zero[:, 0:P], zero[:, :], start=True, stop=False,
                                     skip_group_check=True)
                with pe.Fori(0, nsign) as sg:
                    with pe.Fori(0, NT // 2) as i:
                        for s in range(2):
                            m = (rb * nsign + sg) * (NT // 2) + i
                            n = (rb * nsign + sg) * NT + 2 * i + s
                            pe.wait_ge(at_in[s], m * 16 + 16)
                            pe.wait_ge(a_hi, n + 1)
                            pe.wait_ge(a_lo, n + 3)
                            for h in (HEADS, 0, 1, 2):
                                if h == 0:
                                    pe.wait_ge(a_ph, n + 1)
                                    pe.wait_ge(a_pl, n + 3)
                                hi = Ahi[s][:, :] if h == HEADS else ph[s][:, h, :]
                                lo = Alo[s][:, :] if h == HEADS else pl[s][:, h, :]
                                for w, mv in ((0, hi), (0, lo), (1, hi)):
                                    for q in range(RB // CH):
                                        last = nc.tensor.matmul(psum[:, 2 * h + q, :], Tt[s][:, h, w, :],
                                                                mv[:, q * CH:(q + 1) * CH], start=False,
                                                                stop=False, skip_group_check=True)
                            last.then_inc(a_mm, 1)

            pe.wait_ge(g_in, 48)
            pe.wait_ge(ns_out, NRB + 1)
            pe.wait_ge(es_out, NRB + 1)
            with pe.Fori(0, NC) as q:
                for s in range(2):
                    src = (nsT, esT)[s][:, nlast(q)]
                    hh = hT[:, nlast(q)]
                    pe.wait_ge(g_nin, 2 * q + s + 1)
                    if s == 1:
                        pe.wait_ge(es_ok, q + 1)
                    for g in range(2):
                        nc.tensor.matmul(psum[:, 4 * s + g, :], gruW[:, 2 * s, g * P:(g + 1) * P], src,
                                         start=True, stop=False)
                        nc.tensor.matmul(psum[:, 4 * s + g, :], gruW[:, 2 * s + 1, g * P:(g + 1) * P], hh,
                                         start=False, stop=True)
                    nc.tensor.matmul(psum[:, 4 * s + 2, :], gruW[:, 2 * s, 2 * P:], src, start=True, stop=True)
                    nc.tensor.matmul(psum[:, 4 * s + 3, :], gruW[:, 2 * s + 1, 2 * P:], hh, start=True,
                                     stop=True).then_inc(g_ps, 1)

            def ffn_tensor(k, nE, nF):
                ring, dn, lag = (12, 8)[k], (3, 4)[k], (1, 2)[k]
                pe.wait_ge(r_in, 96 * (k + 1))
                for t in range(NT):
                    if t % 4 == 0:
                        pe.wait_ge(ln_done, 3 + NC * 2 * k + t // 4)
                    last = nc.tensor.matmul(psum[:, 0, NE * t:NE * t + NE], hT[:, t * P:(t + 1) * P], Wr[:, :],
                                            start=(t == 0), stop=True, skip_group_check=True)
                last.then_inc(r_ps, 1)
                pe.wait_ge(r_mask, k + 1)
                for t in range(NT):
                    last = nc.tensor.transpose(flat[0:NE, t * P:(t + 1) * P], s1[:, t, :], ident)
                    if t % 8 == 7:
                        last.then_inc(r_tr, 1)
                pe.wait_ge(r_mk8, 4 * k + 4)
                pe.sem_inc(down_done[k], ring // nF)
                pe.wait_ge(f_lo, 3 * k + 3)
                parts = ((0, 0), (0, 1), (1, 0))

                def up(q, e):
                    for f in range(nF):
                        j = e * nF + f
                        pe.wait_ge(act_done[k], q * (nE * nF) + j + 1)
                        for w, (x, y) in enumerate(parts):
                            last = nc.tensor.matmul(psum[:, j % HB, :], fW[0][x][:, j * P:(j + 1) * P],
                                                    hTp[y][:, nlast(q)], start=(w == 0), stop=(w == 2))
                        last.then_inc(up_done[k], 1)

                def down(q, e):
                    pe.wait_ge(hid_lo[k], q * (nE * nF) + HB + (e + 1) * nF)
                    pe.wait_ge(y_used[k], q * nE + e + 1)
                    for f in range(nF):
                        j = e * nF + f
                        for w, (x, y) in enumerate(parts):
                            last = nc.tensor.matmul(psum[:, HB + e % dn, :], fW[1][x][:, j * P:(j + 1) * P],
                                                    hidp[j % ring][:, y, :], start=(f == 0 and w == 0),
                                                    stop=(f == nF - 1 and w == 2))
                    last.then_inc(down_done[k], 1)

                for e in range(lag):
                    up(0, e)
                with pe.Fori(0, NC - 1) as q:
                    for e in range(nE):
                        up(q + (e + lag) // nE, (e + lag) % nE)
                        down(q, e)
                for e in range(nE):
                    if e + lag < nE:
                        up(NC - 1, e + lag)
                    down(NC - 1, e)

            pe.wait_ge(g_used, 2 * NC + 2)
            lt_tensor(pe, 0)
            ffn_tensor(0, *FFN0)
            pe.wait_ge(y_used[0], NC * FFN0[0] + 3)
            pe.wait_ge(dve_ffn0, NC * (2 * NE + 1))
            lt_tensor(pe, 1)
            pe.wait_ge(b_w_lo, 2)
            for t in range(NT):
                if t % 4 == 0:
                    pe.wait_ge(b_split, t // 4 + 1)
                    pe.wait_ge(ln_done, 2 + 2 * NC)
                for w, (x, y) in enumerate(((0, 0), (0, 1), (1, 0))):
                    last = nc.tensor.matmul(psum[:, 0, K1 * t:K1 * t + K1], h3b[x][:, t * P:(t + 1) * P],
                                            bw1b[y][:, :], start=(t == 0 and w == 0), stop=True,
                                            skip_group_check=True)
            last.then_inc(b_node, 1)
            pe.wait_ge(b_node_ok, 1)
            with pe.Fori(0, NT // 2) as i:
                for s in range(2):
                    n = 2 * i + s
                    pe.wait_ge(b_prod_a, n + 1)
                    pe.wait_ge(b_prod_d, n + 1)
                    for c in range(4):
                        for w, (x, y) in enumerate(((0, 0), (0, 1), (1, 0))):
                            last = nc.tensor.matmul(psum[:, 4 * s + c, :], h3b[x][:, ds(n * P, P)],
                                                    bw2[y][:, c * CH:(c + 1) * CH], start=(w == 0),
                                                    stop=(w == 2))
                    last.then_inc(b_ps, 1)
            pe.wait_ge(b_prod_a, NT + 2)
            pe.wait_ge(b_prod_d, NT + 2)
            pe.wait_ge(b_in, 64)
            nc.tensor.matmul(psum[:, 0, 0:P], bw1T[:, :], bb[:, :], start=True, stop=True).then_inc(b_node, 1)
            pe.wait_ge(b_node_ok, 2)
            for q in range(NC):
                nc.tensor.matmul(psum[:, q, :], wb[:, :], hT[:, q * CH:(q + 1) * CH], start=True, stop=False,
                                 skip_group_check=True)
            pe.wait_ge(b_x, NT + 2)
            pe.sem_inc(l_mm, 4)
            with pe.Fori(0, NT // 4) as i:
                for s in range(4):
                    n = 4 * i + s
                    pe.wait_ge(l_hi, n + 1)
                    pe.wait_ge(l_lo, n + 1)
                    for w, mv in ((0, A4hi), (0, A4lo), (1, A4hi)):
                        for q in range(NC):
                            last = nc.tensor.matmul(psum[:, q, :], Xb[w][:, ds(n, 1), :].rearrange("p o f -> p (o f)"),
                                                    mv[s][:, q * CH:(q + 1) * CH], start=False, stop=False,
                                                    skip_group_check=True)
                    last.then_inc(l_mm, 1)
            pe.wait_ge(l_add, NC)
            lt_tensor(pe, 2)
            ffn_tensor(1, *FFN1)

        @block.vector
        def _(dve):
            V = nc.vector
            c = Chain(dve, dve_steps)

            def inverse_root(t):
                c.link(V.reciprocal(stat[:, 4, t], stat[:, 3, t]))
                c.link(V.tensor_tensor(stat[:, 5, t], stat[:, 4, t], stat[:, 4, t], ALU.mult))
                c.link(V.tensor_tensor(stat[:, 5, t], stat[:, 5, t], stat[:, 2, t], ALU.mult))
                c.link(V.tensor_scalar(stat[:, 5, t], stat[:, 5, t], -0.5, 1.5, ALU.mult, ALU.add))
                return V.tensor_tensor(stat[:, 4, t], stat[:, 4, t], stat[:, 5, t], ALU.mult)

            def ln_vector():
                for hf in range(2):
                    t = slice(16 * hf, 16 * hf + 16)
                    ps = flat[:, hf * N // 2:(hf + 1) * N // 2].rearrange("p (t f) -> p t f", f=P)
                    wide = [P, 16, P]
                    dve.wait_ge(ln_turned, hf + 1)
                    c.link(V.tensor_reduce(stat[:, 0, t], ps, AX, ALU.add))
                    c.link(V.tensor_scalar(stat[:, 1, t], stat[:, 0, t], 1.0 / P, None, ALU.mult))
                    V.tensor_tensor(hn[:, t, :], ps, stat[:, 1, t].unsqueeze(2).to_broadcast(wide),
                                    ALU.subtract).then_inc(ln_centred, 1)
                for hf in range(2):
                    t = slice(16 * hf, 16 * hf + 16)
                    dve.wait_ge(ln_squared, hf + 1)
                    c.link(V.tensor_reduce(stat[:, 0, t], sq[:, :, :], AX, ALU.add))
                    V.tensor_scalar(stat[:, 2, t], stat[:, 0, t], 1.0 / P, EPS, ALU.mult, ALU.add).then_inc(ln_var, 1)
                    dve.wait_ge(ln_std, hf + 1)
                    dve.wait_ge(ln_var, hf + 1)
                    dve.wait_ge(ln_centred, hf + 1)
                    c.link(inverse_root(t))
                    V.tensor_tensor(hn[:, t, :], hn[:, t, :], stat[:, 4, t].unsqueeze(2).to_broadcast([P, 16, P]),
                                    ALU.mult).then_inc(ln_normed, 1)

            def lt_vector(k):
                for q in range(NC):
                    xq = slice(q * CH, (q + 1) * CH)
                    dve.wait_ge(lt_mean, NC * k + q + 1)
                    V.tensor_tensor(hc[:, xq], xT[:, xq], psum[:, q, :], ALU.subtract).then_inc(lt_centred, 1)
                dve.wait_ge(lt_sum, NC * (k + 1))
                V.tensor_scalar(stat[:, 2, :], psum[:, 0, 0:NT], EPS, None, ALU.add).then_inc(ln_var, 1)
                dve.wait_ge(ln_std, 3 + k)
                inverse_root(slice(0, NT)).then_inc(ln_normed, 1)
                for q in range(NC):
                    xq = slice(q * CH, (q + 1) * CH)
                    dve.wait_ge(ln_back, 3 + NC * k + q)
                    V.tensor_tensor(hT[:, xq], hc[:, xq], psum[:, q, :], ALU.mult).then_inc(ln_done, 1)

            dve.wait_ge(cst_in, 16)
            c.link(V.memset(zero[:, :], 0.0))
            c.link(V.tensor_copy(selC[:, :], selCf))
            ln_vector()
            dve.wait_ge(uv_ps, 1)
            V.tensor_copy(wa[:, :, :], psum[:, 0, 0:6].rearrange("p (h a) -> p a h", a=2)).then_inc(uv_ok, 1)
            dve.wait_ge(uv_ps, 2)
            ps = psum[:, 1, 0:6 * NT].rearrange("p (t x) -> p t x", x=6)
            c.link(V.tensor_copy(uvs[:, :, 0, :], ps))
            c.link(V.tensor_tensor(uvr[:, :, :], ps, uvs[:, :, 0, :], ALU.subtract))
            c.link(V.tensor_copy(uvs[:, :, 1, :], uvr[:, :, :]))
            c.link(V.tensor_tensor(uvr[:, :, :], uvr[:, :, :], uvs[:, :, 1, :], ALU.subtract))
            c.link(V.tensor_copy(uvs[:, :, 2, :], uvr[:, :, :]))
            for part in range(3):
                c.link(V.tensor_copy(uvx[:, :, part, 0:3], uvs[:, :, part, 3:6]))
                c.link(V.tensor_copy(uvx[:, :, part, 3:6], uvs[:, :, part, 0:3]))
            V.memset(sm[:, :], 0.0).then_inc(uv_ok, 1)
            dve.wait_ge(uv_ok, 2)
            dve.wait_ge(spilled, 48)

            dve.sem_inc(m_mask, 1)
            with dve.Fori(0, NT // 2) as i:
                for s in range(2):
                    n = 2 * i + s
                    blk = Ar[s][:, ds(n * P, P)]
                    dve.wait_ge(m_in[s], i * 16 + 16)
                    V.tensor_tensor(blk, blk, offd, ALU.mult).then_inc(m_diag, 1)
                    dve.wait_ge(m_diag, n + 1)
                    dve.wait_ge(m_sum, n + 1)
                    V.tensor_scalar(Pb[s][:, :], Ar[s][:, :], 0.0, None, ALU.is_gt).then_inc(m_mask, 1)
                    dve.wait_ge(m_mask, n + 2)
                    V.tensor_copy(keep[:, ds(n * N, N)], Pb[s][:, :]).then_inc(m_kept, 1)
            dve.wait_ge(m_neg, NT + 1)
            V.tensor_reduce(sm[:, 9:10], negs[:, :], AX, ALU.add).then_inc(neg_rows, 1)
            dve.wait_ge(neg_tot, 1)
            c.link(V.tensor_scalar(sm[:, 10:11], psum[:, 2, 0:1], 0.0, None, ALU.is_gt))
            c.link(V.tensor_scalar(sm[:, 11:12], sm[:, 10:11], 1.0, None, ALU.add))
            c.link(V.tensor_scalar(sm[:, 12:13], sm[:, 10:11], -1.0, 1.0, ALU.mult, ALU.add))
            c.link(V.tensor_copy(nsg[:, 2:3], sm[:, 10:11]))
            V.tensor_copy(nsg[:, 0:1], sm[:, 11:12]).then_inc(nsign_ok, 1)
            dve.wait_ge(nsign_ok, 1)
            nsign = dve.value_load(nsg[0:1, 0:1], min_val=1, max_val=2)
            dve.wait_ge(m_kept, NT)
            dve.sem_inc(x_mask, 1)
            with dve.If(nsign == 2):
                with dve.Fori(0, NT) as t:
                    blk = Ar[0][:, ds(t * P, P)]
                    dve.wait_ge(x_in2, t * 16 + 16)
                    V.tensor_tensor(blk, blk, offd, ALU.mult).then_inc(x_diag, 1)
                    dve.wait_ge(x_diag, t + 1)
                    dve.wait_ge(x_sum, t + 1)
                    V.tensor_scalar(Pb[0][:, :], Ar[0][:, :], 0.0, None, ALU.is_lt).then_inc(x_mask, 1)
                dve.wait_ge(x_sum, NT + 1)
            dve.wait_ge(m_sum, NT + 2)
            c.link(V.tensor_copy(zs[:, 0:16, :], psum[:, 0, 0:288].rearrange("p (t x) -> p t x", x=18)))
            c.link(V.tensor_copy(zs[:, 16:32, :], psum[:, 1, 0:288].rearrange("p (t x) -> p t x", x=18)))
            c.link(V.tensor_tensor(z6[:, :, :], zs[:, :, 12:18], zs[:, :, 6:12], ALU.add))
            c.link(V.tensor_tensor(z6[:, :, :], z6[:, :, :], zs[:, :, 0:6], ALU.add))
            z4 = z6[:, :, :].rearrange("p t (s h) -> p t s h", s=2)
            for sg in range(2):
                e3 = e6[:, sg, :].rearrange("p (t h) -> p t h", h=HEADS)
                c.link(V.scalar_tensor_tensor(out=e3, in0=z4[:, :, sg, :], scalar=SLOPE, in1=z4[:, :, sg, :],
                                              op0=ALU.mult, op1=ALU.max))
            c.link(V.tensor_scalar(f6[:, 0, :], e6[:, 0, :], sm[:, 12:13], None, ALU.mult))
            c.link(V.scalar_tensor_tensor(out=e6[:, 1, :], in0=e6[:, 1, :], scalar=sm[:, 10:11], in1=f6[:, 0, :],
                                          op0=ALU.mult, op1=ALU.add))
            c.link(V.tensor_scalar(q6[:, :, :], e6[:, :, :], 1.0 / LN2, None, ALU.mult))
            c.link(V.tensor_scalar(q6[:, :, :], q6[:, :, :], ROUND, None, ALU.add))
            c.link(V.tensor_scalar(q6[:, :, :], q6[:, :, :], -ROUND, None, ALU.add))
            c.link(V.scalar_tensor_tensor(out=f6[:, :, :], in0=q6[:, :, :], scalar=-LN2_HI, in1=e6[:, :, :],
                                          op0=ALU.mult, op1=ALU.add))
            V.scalar_tensor_tensor(out=f6[:, :, :], in0=q6[:, :, :], scalar=-LN2_LO, in1=f6[:, :, :],
                                   op0=ALU.mult, op1=ALU.add).then_inc(frac_ok, 1)
            V.tensor_reduce(sm[:, 0:3], q6[:, :, :].rearrange("p s (t h) -> p h (s t)", h=HEADS), AX,
                            ALU.max).then_inc(range_l, 1)
            dve.wait_ge(range_g, 1)
            for sg in range(2):
                d3 = dpt[:, sg * NT * HEADS:(sg + 1) * NT * HEADS].rearrange("p (t h) -> p t h", h=HEADS)
                c.link(V.tensor_tensor(d3, q6[:, sg, :].rearrange("p (t h) -> p t h", h=HEADS),
                                       sm[:, 3:6].unsqueeze(1).to_broadcast([P, NT, HEADS]), ALU.subtract))
            c.link(V.tensor_scalar(dpt[:, :], dpt[:, :], 1.0 / LEVEL, None, ALU.mult))
            c.link(V.tensor_reduce(sm[:, 8:9], dpt[:, :], AX, ALU.min))
            V.tensor_scalar(sm[:, 6:7], sm[:, 8:9], -1.0, None, ALU.mult).then_inc(range_l, 1)
            dve.wait_ge(range_g, 2)
            c.link(V.tensor_scalar(sm[:, 13:14], sm[:, 7:8], 1.0 / KL, 0.51, ALU.mult, ALU.add))
            c.link(V.tensor_scalar(sm[:, 13:14], sm[:, 13:14], 1.0, None, ALU.max))
            c.link(V.tensor_copy(lev[:, :], kk))
            c.link(V.memset(acc6[:, :], 0.0))
            c.link(V.memset(lw[:, :, 2 * PART:P], 0.0))
            V.tensor_copy(nsg[:, 1:2], sm[:, 13:14]).then_inc(groups_ok, 1)
            dve.wait_ge(groups_ok, 1)
            dve.wait_ge(wm_ok, 1)
            groups = dve.value_load(nsg[0:1, 1:2], min_val=1, max_val=1 << 20)

            LVSTEPS = 8
            dve.sem_inc(ly_mask, 1)
            dve.sem_inc(lv_ind, 1)

            def level_weights(l, sg, cap, exp, nexp, last):
                dp = dpt[:, sg * NT * HEADS:(sg + 1) * NT * HEADS].unsqueeze(2).to_broadcast([P, NT * HEADS, KL])
                w = wm[:, sg * NT * HEADS:(sg + 1) * NT * HEADS].unsqueeze(2).to_broadcast([P, NT * HEADS, KL])
                lb = lev[:, :].unsqueeze(1).to_broadcast([P, NT * HEADS, KL])
                l.link(V.tensor_tensor(lvU[:, :, :], dp, lb, ALU.add))
                V.tensor_scalar(lvE[:, :, :], lvU[:, :, :], 0.0, None, ALU.min).then_inc(cap, 1)
                l.link(V.tensor_scalar(lvP[:, :, :], lvU[:, :, :], 0.0, POISON, ALU.is_gt, ALU.mult))
                dve.wait_ge(exp, nexp)
                l.link(V.tensor_tensor(lvW[:, :, :], lvE[:, :, :], w, ALU.mult))
                l.link(V.tensor_tensor(lvW[:, :, :], lvW[:, :, :], lvP[:, :, :], ALU.add))
                W = lvW[:, :, :].rearrange("p (t h) k -> p t (h k)", h=HEADS)
                U = lvU[:, :, :].rearrange("p (t h) k -> p t (h k)", h=HEADS)
                PZ = lvP[:, :, :].rearrange("p (t h) k -> p t (h k)", h=HEADS)
                l.link(V.tensor_copy(lw[:, :, 0:PART], W))
                l.link(V.tensor_tensor(U, W, lw[:, :, 0:PART], ALU.subtract))
                V.tensor_tensor(lw[:, :, PART:2 * PART], U, PZ, ALU.add).then_inc(last, 1)

            with dve.Fori(0, groups) as g:
                l = Chain(dve, dve_lv, g * LVSTEPS)
                level_weights(l, 0, lv_cap, lv_exp, g + 1, lv_w)
                with dve.Fori(0, NT // 4) as i:
                    for s in (0, 2):
                        dve.wait_ge(lv_w, g + 1)
                        dve.wait_ge(lv_sum, g * NT + 4 * i + s + 1)
                        V.tensor_copy(Pb[s][:, :], keep[:, ds((4 * i + s) * N, N)]).then_inc(lv_conv0, 1)
                with dve.If(nsign == 2):
                    dve.wait_ge(lv_sum, (g + 1) * NT + 4)
                    level_weights(Chain(dve, dve_ly, g * 6), 1, ly_cap, ly_exp, g + 1, ly_w)
                    with dve.Fori(0, NT) as t:
                        blk = Ar[0][:, ds(t * P, P)]
                        dve.wait_ge(ly_in, (g * NT + t) * 16 + 16)
                        V.tensor_tensor(blk, blk, offd, ALU.mult).then_inc(ly_diag, 1)
                        dve.wait_ge(ly_diag, g * NT + t + 1)
                        dve.wait_ge(ly_sum, g * NT + t + 1)
                        V.tensor_scalar(Pb[0][:, :], Ar[0][:, :], 0.0, None, ALU.is_lt).then_inc(ly_mask, 1)
                dve.wait_ge(lv_all, g + 1)
                l.link(V.tensor_copy(lsum[:, N // 2:], flat[:, N // 2:]))
                l.link(V.tensor_scalar(lev[:, :], lev[:, :], float(KL), None, ALU.add))
                dve.wait_ge(lv_copied, g + 1)
                V.tensor_scalar(lind[:, :], lsum[:, :], CLEAN, None, ALU.is_lt).then_inc(lv_ind, 1)
                V.scalar_tensor_tensor(out=lsum[:, :], in0=lsum[:, :], scalar=CLEAN, in1=lsum[:, :],
                                       op0=ALU.is_lt, op1=ALU.mult).then_inc(lv_ind, 1)
                dve.wait_ge(lv_sel, g + 1)
                V.tensor_tensor(acc6[:, :], acc6[:, :], flat[0:6, :], ALU.add).then_inc(lv_ind, 1)
                dve.wait_ge(lv_ind, 3 * g + 4)
                assert l.n == LVSTEPS, l.n
            V.tensor_scalar(kr16[:, :], acc6[:, :], -1.0, 30000.0, ALU.add, ALU.min).then_inc(kr_ok, 1)

            dve.sem_inc(t_lo, TS)
            dve.sem_inc(t_mul, TS)
            with dve.Fori(0, nsign) as sg:
                def scaled(t, s):
                    dve.wait_ge(t_ps, sg * NT + t + 1)
                    dve.wait_ge(t_lo, sg * NT + t + 1)
                    V.scalar_tensor_tensor(
                        out=tf[s][:, 0:HEADS, :], in0=psum[:, s, 0:HEADS * P].rearrange("p (h f) -> p h f", f=P),
                        scalar=sgn[:, ds(sg, 1)],
                        in1=wm[:, ds((sg * NT + t) * HEADS, HEADS)].unsqueeze(2).to_broadcast([P, HEADS, P]),
                        op0=ALU.mult, op1=ALU.mult).then_inc(t_mul, 1)

                def low(t, s):
                    dve.wait_ge(t_hi, sg * NT + t + 1)
                    V.tensor_tensor(tb[s][:, :, 1, :], tf[s][:, :, :], tb[s][:, :, 0, :],
                                    ALU.subtract).then_inc(t_lo, 1)

                scaled(0, 0)
                with dve.Fori(0, NT // TS - 1) as i:
                    for s in range(TS):
                        scaled(TS * i + s + 1, (s + 1) % TS)
                        low(TS * i + s, s)
                for s in range(TS):
                    if s < TS - 1:
                        scaled(NT - TS + s + 1, s + 1)
                    low(NT - TS + s, s)

            dve.wait_ge(den_back, 16)
            c.link(V.tensor_scalar(den96[:, :], den96[:, :], TINY, None, ALU.max))
            c.link(V.reciprocal(den96[:, :], den96[:, :]))
            V.tensor_scalar(den96[:, :], den96[:, :], 1.0 / HEADS, None, ALU.mult).then_inc(rden_ok, 1)
            dve.wait_ge(kr_out, 32)
            dve.sem_inc(a_pl, 2)
            dve.sem_inc(es_out, 1)
            with dve.Fori(0, NRB) as rb:
                def scale(sg, t, s, n):
                    dve.wait_ge(a_s, n + 1)
                    for h in range(HEADS):
                        last = V.tensor_scalar(tt[s][:, h, :], KR[:, h, ds(rb * RB, RB)],
                                               dpt[:, ds((sg * NT + t) * HEADS + h, 1)], 0.0, ALU.add, ALU.min)
                    last.then_inc(a_t, 1)

                def parts(s, n):
                    dve.wait_ge(a_s, n + 3)
                    dve.wait_ge(a_hi, n + 1)
                    dve.wait_ge(a_mm, n + 1)
                    V.tensor_tensor(ph[s][:, :, :], ss[s][:, :, :],
                                    Ahi[s][:, :].unsqueeze(1).to_broadcast([P, HEADS, RB]), ALU.mult).then_inc(a_ph, 1)
                    dve.wait_ge(a_lo, n + 3)
                    V.tensor_tensor(pl[s][:, :, :], ss[s][:, :, :],
                                    Alo[s][:, :].unsqueeze(1).to_broadcast([P, HEADS, RB]), ALU.mult).then_inc(a_pl, 1)

                with dve.Fori(0, nsign) as sg:
                    n0 = (rb * nsign + sg) * NT
                    scale(sg, 0, 0, n0)
                    with dve.Fori(0, NT // 2 - 1) as i:
                        for s in range(2):
                            scale(sg, 2 * i + s + 1, 1 - s, n0 + 2 * i + s + 1)
                            parts(s, n0 + 2 * i + s)
                    scale(sg, NT - 1, 1, n0 + (NT - 1))
                    parts(0, n0 + (NT - 2))
                    parts(1, n0 + (NT - 1))
                dve.wait_ge(a_mm, (rb + 1) * nsign * NT + 2)
                dve.wait_ge(rd_in, rb * 48 + 48)
                V.tensor_tensor(esP[:, :, ds(rb * RB, RB)],
                                flat[:, 0:HEADS * RB].rearrange("p (h r) -> p h r", h=HEADS), RD[:, :, :],
                                ALU.mult).then_inc(es_out, 1)

            dve.wait_ge(g_in, 48)
            for s in range(2):
                V.tensor_tensor(gbr[:, s, :], gruB[:, 2 * s, 0:2], gruB[:, 2 * s + 1, 0:2],
                                ALU.add).then_inc(gbr_ok, 1)
            dve.sem_inc(g_nin, 2)
            dve.sem_inc(g_new, 2)

            def reset(q, s, n):
                gc = Chain(dve, dve_gru, n)
                dve.wait_ge(g_new, n + 1)
                dve.wait_ge(g_gate, n * 2 + 2)
                gc.link(V.scalar_tensor_tensor(out=gM[s][:, :], in0=psum[:, 4 * s + 3, :],
                                               scalar=gruB[:, 2 * s + 1, 2:3], in1=gR[s][:, :], op0=ALU.add,
                                               op1=ALU.mult))
                V.tensor_tensor(gM[s][:, :], gM[s][:, :], psum[:, 4 * s + 2, :], ALU.add).then_inc(g_nin, 1)

            def update(q, s, n):
                gc = Chain(dve, dve_upd, 2 * n)
                dve.wait_ge(g_tanh, n + 1)
                dve.wait_ge(g_used, n + 1)
                gc.link(V.tensor_tensor(gU[s][:, :], hT[:, nlast(q)], gM[s][:, :], ALU.subtract))
                gc.link(V.tensor_tensor(gU[s][:, :], gU[s][:, :], gZ[s][:, :], ALU.mult))
                V.tensor_tensor(gU[s][:, :], gU[s][:, :], gM[s][:, :], ALU.add).then_inc(g_new, 1)

            reset(0, 0, 0)
            with dve.Fori(0, NC - 1) as q:
                for s in range(2):
                    reset(q + s, 1 - s, 2 * q + s + 1)
                    update(q, s, 2 * q + s)
            reset(NC - 1, 1, 2 * NC - 1)
            update(NC - 1, 0, 2 * NC - 2)
            update(NC - 1, 1, 2 * NC - 1)

            def ffn_vector(k, nE, nF):
                dn = (3, 4)[k]
                T = [P, NT, NE]
                dve.wait_ge(r_ps, k + 1)
                ps = psum[:, 0, 0:NT * NE].rearrange("p (t e) -> p t e", e=NE)
                c.link(V.tensor_tensor(lg[:, :, :], ps, rb2[:, 0, :].unsqueeze(1).to_broadcast(T), ALU.add))
                c.link(V.tensor_tensor(lg[:, :, :], lg[:, :, :], rb2[:, 1, :].unsqueeze(1).to_broadcast(T), ALU.add))
                for r, sel in enumerate((s1, s2)):
                    c.link(V.tensor_reduce(rs[:, r, :], lg[:, :, :], AX, ALU.max))
                    c.link(V.tensor_tensor(rq[:, :, :], lg[:, :, :], rs[:, r, :].unsqueeze(2).to_broadcast(T),
                                           ALU.is_equal))
                    c.link(V.tensor_tensor(rq[:, :, :], rq[:, :, :], prio.unsqueeze(1).to_broadcast(T), ALU.mult))
                    c.link(V.tensor_reduce(rs[:, 4, :], rq[:, :, :], AX, ALU.max))
                    c.link(V.tensor_tensor(sel[:, :, :], rq[:, :, :], rs[:, 4, :].unsqueeze(2).to_broadcast(T),
                                           ALU.is_equal))
                    if r == 0:
                        c.link(V.scalar_tensor_tensor(out=lg[:, :, :], in0=s1[:, :, :], scalar=-1e30,
                                                      in1=lg[:, :, :], op0=ALU.mult, op1=ALU.add))
                V.tensor_tensor(rs[:, 2, :], rs[:, 1, :], rs[:, 0, :], ALU.subtract).then_inc(r_gap, 1)
                dve.wait_ge(r_exp, k + 1)
                c.link(V.tensor_scalar(rs[:, 5, :], rs[:, 3, :], 1.0, None, ALU.add))
                c.link(V.reciprocal(rs[:, 6, :], rs[:, 5, :]))
                c.link(V.tensor_tensor(rs[:, 7, :], rs[:, 6, :], rs[:, 3, :], ALU.mult))
                c.link(V.tensor_tensor(s1[:, :, :], s1[:, :, :], rs[:, 6, :].unsqueeze(2).to_broadcast(T), ALU.mult))
                c.link(V.tensor_tensor(s2[:, :, :], s2[:, :, :], rs[:, 7, :].unsqueeze(2).to_broadcast(T), ALU.mult))
                V.tensor_tensor(s1[:, :, :], s1[:, :, :], s2[:, :, :], ALU.add).then_inc(r_mask, 1)
                fsem, per = (dve_ffn0, dve_ffn1)[k], 2 * NE + (nE - NE)
                credits, hold, ring, lag = dn, (3, 4)[k], (12, 8)[k], (1, 2)[k]
                dve.sem_inc(y_used[k], credits)
                dve.wait_ge(f_lo, 3 * k + 3)

                def high(q, e):
                    for j in range(e * nF, (e + 1) * nF):
                        dve.wait_ge(act_done[k], q * (nE * nF) + HB + j + 1)
                        dve.wait_ge(down_done[k], q * nE + e + 1)
                        V.tensor_copy(hidp[j % ring][:, 0, :], hid[j % HB][:, :]).then_inc(hid_hi[k], 1)

                def weighted(q, i, half, e, f):
                    xq = xT[:, nlast(q)]
                    if e == nE - NE:
                        dve.wait_ge(mB_in[k][half], (i + 1) * (16 * NE))
                    dve.wait_ge(down_done[k], q * nE + hold + e + 1)
                    y = psum[:, HB + e % dn, :]
                    if e < nE - NE:
                        f.link(V.scalar_tensor_tensor(out=xq, in0=y, scalar=fB2[:, e:e + 1], in1=xq,
                                                      op0=ALU.add, op1=ALU.add))
                    else:
                        f.link(V.scalar_tensor_tensor(out=yT[e % 2][:, :], in0=y, scalar=fB2[:, e:e + 1],
                                                      in1=mB[:, half * NE + e - (nE - NE), :], op0=ALU.add,
                                                      op1=ALU.mult))
                        f.link(V.tensor_tensor(xq, xq, yT[e % 2][:, :], ALU.add))
                    dve.sem_inc(y_used[k], 1)

                def chunk(q, i, half, more):
                    f = Chain(dve, fsem, q * per)
                    for e in range(nE):
                        if e + lag < nE or more:
                            high(q + (e + lag) // nE, (e + lag) % nE)
                        weighted(q, i, half, e, f)
                    assert f.n == per

                for e in range(lag):
                    high(0, e)
                with dve.Fori(0, NC // 2 - 1) as i:
                    for half in range(2):
                        chunk(2 * i + half, i, half, True)
                chunk(NC - 2, NC // 2 - 1, 0, True)
                chunk(NC - 1, NC // 2 - 1, 1, False)

            lt_vector(0)
            ffn_vector(0, *FFN0)
            lt_vector(1)
            for q in range(NC):
                c_q = slice(q * CH, (q + 1) * CH)
                dve.wait_ge(b_hi, q + 3)
                V.tensor_tensor(h3b[1][:, c_q], hT[:, c_q], h3b[0][:, c_q], ALU.subtract).then_inc(b_split, 1)
            dve.wait_ge(b_node, 1)
            V.tensor_copy(nodek[:, :, :], psum[:, 0, :].rearrange("p (t k) -> p t k", k=K1)).then_inc(b_node_ok, 1)
            dve.wait_ge(b_node_ok, 1)
            dve.sem_inc(b_prod_d, 2)
            dve.sem_inc(b_sum, 2)

            def products(n, s):
                dve.wait_ge(b_ps, n + 1)
                dve.wait_ge(b_half, n + 1)
                V.tensor_tensor(prod[s][:, K1 // 2:, :],
                                psum[:, 4 * s + 2:4 * s + 4, :].rearrange("p b (k f) -> p (b k) f", f=P),
                                nodek[:, ds(n, 1), K1 // 2:].rearrange("p o k -> p (o k)").unsqueeze(2)
                                .to_broadcast([P, K1 // 2, P]), ALU.mult).then_inc(b_prod_d, 1)

            def summed(n, s):
                dve.wait_ge(b_half, n + 3)
                dve.wait_ge(b_x, n + 1)
                V.tensor_reduce(xf[s][:, :], halves[s][:, :, :].rearrange("p k f -> p f k"), AX,
                                ALU.add).then_inc(b_sum, 1)
                dve.wait_ge(b_sum, n + 3)
                V.tensor_copy(Xb[0][:, ds(n, 1), :].rearrange("p o f -> p (o f)"), xf[s][:, :]).then_inc(b_x_hi, 1)

            products(0, 0)
            with dve.Fori(0, NT // 2 - 1) as i:
                for s in range(2):
                    products(2 * i + s + 1, 1 - s)
                    summed(2 * i + s, s)
            products(NT - 1, 1)
            summed(NT - 2, 0)
            summed(NT - 1, 1)
            dve.wait_ge(b_node, 2)
            V.tensor_copy(wb[:, :], psum[:, 0, 0:P]).then_inc(b_node_ok, 1)
            with dve.Fori(0, NT // 4) as i:
                for s in range(4):
                    dve.wait_ge(l_hi, 4 * i + s + 1)
                    dve.wait_ge(l_mm, 4 * i + s + 1)
                    V.tensor_tensor(A4lo[s][:, :], A4[s][:, :], A4hi[s][:, :], ALU.subtract).then_inc(l_lo, 1)
            dve.wait_ge(l_mm, NT + 4)
            for q in range(NC):
                xq = xT[:, q * CH:(q + 1) * CH]
                V.scalar_tensor_tensor(out=xq, in0=psum[:, q, :], scalar=0.0, in1=xq, op0=ALU.max,
                                       op1=ALU.add).then_inc(l_add, 1)
            dve.wait_ge(l_add, NC)
            lt_vector(2)
            ffn_vector(1, *FFN1)


def kernel(**inputs):
    import numpy as np
    import concourse.bacc as bacc
    from concourse import mybir as mb
    from concourse.bass_utils import run_bass_kernel_spmd as run

    g = {k: np.asarray(v) for k, v in inputs.items()}

    def tiles_last(b, n):
        return b.reshape(n, P).T

    def expert_w1(w):
        return w.transpose(1, 0, 2).reshape(P, -1)

    def expert_w2(w):
        e, f, d = w.shape
        return w.reshape(e, f // P, P, d).transpose(2, 0, 1, 3).reshape(P, -1)

    consts = np.zeros((P, C_END), np.float32)
    consts[:, C_ID:C_ID + P] = np.eye(P)
    consts[:, C_OFF:C_OFF + P] = 1 - np.eye(P)
    consts[:, C_ONE:C_ONE + P] = 1
    for h in range(HEADS):
        for part in range(2):
            rows = slice(part * PART + h * KL, part * PART + (h + 1) * KL)
            consts[rows, C_SD + 3 + h] = 1
            if part == 0:
                consts[rows, C_SC + h] = 1
    consts[:, C_AV:] = 1 / P
    consts[:, C_KK:C_KK + KL] = np.arange(KL)
    consts[:, C_PR:C_PR + NE] = NE - np.arange(NE)
    consts[:, C_SG], consts[:, C_SG + 1] = 1, -1

    p0, p1, q0, q1 = "L0_gnn_", "L0_ffn_", "L1_gnn_", "L1_ffn_"
    arrays = {
        "consts": consts,
        "xT": g["x"].T,
        "adjT": g["adj"].T,
        "gatW": g[p0 + "gat_W"].transpose(1, 0, 2).reshape(P, -1),
        "gatWT": g[p0 + "gat_W"].transpose(2, 0, 1).reshape(P, -1),
        "gatA": g[p0 + "gat_a"].reshape(HEADS, 2, P).transpose(2, 0, 1),
        "gruW": np.stack([g[p0 + n].T for n in ("edge_Wih", "edge_Whh", "node_Wih", "node_Whh")], 1),
        "gruB": np.stack([tiles_last(g[p0 + n], 3) for n in ("edge_bih", "edge_bhh", "node_bih", "node_bhh")], 1),
        "Wr_0": g[p1 + "Wr"],
        "rb_0": np.zeros((2, NE), np.float32),
        "W1_0": np.concatenate([g[p1 + "W1s"], expert_w1(g[p1 + "W1p"])], 1),
        "W2_0": np.concatenate([expert_w2(g[p1 + "W2s"][None]), expert_w2(g[p1 + "W2p"])], 1),
        "B1_0": np.concatenate([tiles_last(g[p1 + "b1s"], 4), tiles_last(g[p1 + "b1p"].reshape(-1), 32)], 1),
        "B2_0": np.concatenate([g[p1 + "b2s"][:, None], g[p1 + "b2p"].T], 1),
        "b_W1": g[q0 + "W1"],
        "b_W1T": g[q0 + "W1"].T,
        "b_W2": g[q0 + "W2"].transpose(1, 0, 2).reshape(P, -1),
        "b_b": g[q0 + "b"],
        "Wr_1": g[q1 + "Wg"],
        "rb_1": np.stack([g[q1 + "bg"], g[q1 + "bias"]]),
        "W1_1": expert_w1(g[q1 + "W1"]),
        "W2_1": expert_w2(g[q1 + "W2"]),
        "B1_1": tiles_last(g[q1 + "b1"].reshape(-1), 16),
        "B2_1": g[q1 + "b2"].T,
    }
    nc = bacc.Bacc("TRN2", target_bir_lowering=False, num_devices=1)
    sent, aps = {}, {}
    for name, v in arrays.items():
        v = np.ascontiguousarray(v)
        sent["in_" + name] = v
        aps[name] = nc.dram_tensor("in_" + name, v.shape, mb.dt.from_np(v.dtype), kind="ExternalInput").ap()
    out = nc.dram_tensor("out_xT", (P, N), F32, kind="ExternalOutput").ap()
    build(nc, aps, out)
    r = run(nc, [sent], core_ids=[0])
    return np.ascontiguousarray(r.results[0]["out_xT"].T)
```
